# Optimizing a Trainium2 kernel written in Bass

```python
import numpy as np
import jax
import jax.numpy as jnp

def _softmax(x, axis=-1):
    return jax.nn.softmax(x, axis=axis)
def _gelu(x):
    return jax.nn.gelu(x, approximate=True)
def _silu(x):
    return jax.nn.silu(x)
def _sigmoid(x):
    return jax.nn.sigmoid(x)
def _layernorm(x, axis=-1, eps=1e-5):
    m = jnp.mean(x, axis=axis, keepdims=True)
    v = jnp.var(x, axis=axis, keepdims=True)
    return (x - m) / jnp.sqrt(v + eps)
def _scatter_add(tgt, idx, src, axis=0):
    return tgt.at[idx].add(src)
def _segment_sum(src, seg, n):
    return jax.ops.segment_sum(src, seg, n)

kernel_name = 'mk_conv_seq_d1_conv_nchw192_0fdf91'

def setup_inputs(seed: int = 0):
    np.random.seed(seed)
    _w = jnp.asarray
    def _rec_inputs():
        import jax
        import jax.numpy as jnp
        _gk = jax.random.key(seed)
        x = 7.572e-06 + 1 * jax.random.normal(jax.random.fold_in(_gk, 1), (16, 192, 56, 56), jnp.float32)
        return x
    x = _rec_inputs()
    def _L0_conv_setup():
        import jax, jax.numpy as jnp
        import numpy as np
        DIM = 192
        HEADS = 6
        HD = DIM // HEADS
        WS = 7
        N = WS * WS
        SHIFT = 3
        HID = 768
        EPS = 1e-05
        SCALE = HD ** (-0.5)

        def _rel_pos_index():
            coords = np.stack(np.meshgrid(np.arange(WS), np.arange(WS), indexing='ij'))
            cf = coords.reshape(2, -1)
            rc = (cf[:, :, None] - cf[:, None, :]).transpose(1, 2, 0)
            rc[:, :, 0] += WS - 1
            rc[:, :, 1] += WS - 1
            rc[:, :, 0] *= 2 * WS - 1
            return rc.sum(-1)
        REL_IDX = jnp.asarray(_rel_pos_index().reshape(-1))

        def _attn_mask(H, W):
            img = np.zeros((H, W))
            sl = (slice(0, -WS), slice(-WS, -SHIFT), slice(-SHIFT, None))
            cnt = 0
            for hs in sl:
                for ws_ in sl:
                    img[hs, ws_] = cnt
                    cnt += 1
            m = img.reshape(H // WS, WS, W // WS, WS).transpose(0, 2, 1, 3).reshape(-1, N)
            diff = m[:, None, :] - m[:, :, None]
            return jnp.asarray(np.where(diff != 0, -100.0, 0.0).astype(np.float32))

        def _ln(x, g, b):
            mu = x.mean(-1, keepdims=True)
            var = ((x - mu) ** 2).mean(-1, keepdims=True)
            return (x - mu) * jax.lax.rsqrt(var + EPS) * g + b
        key = jax.random.key(seed)
        ks = jax.random.split(key, 8)
        s = 0.02
        return {'x': jax.random.normal(ks[0], (16, DIM, 56, 56), jnp.float32), 'qkv_w': jax.random.normal(ks[1], (3 * DIM, DIM), jnp.float32) * s, 'qkv_b': jnp.zeros((3 * DIM,), jnp.float32), 'proj_w': jax.random.normal(ks[2], (DIM, DIM), jnp.float32) * s, 'proj_b': jnp.zeros((DIM,), jnp.float32), 'rpb_table': jax.random.normal(ks[3], ((2 * WS - 1) ** 2, HEADS), jnp.float32) * s, 'norm1_g': jnp.ones((DIM,), jnp.float32), 'norm1_b': jnp.zeros((DIM,), jnp.float32), 'norm2_g': jnp.ones((DIM,), jnp.float32), 'norm2_b': jnp.zeros((DIM,), jnp.float32), 'fc1_w': jax.random.normal(ks[4], (HID, DIM), jnp.float32) * s, 'fc1_b': jnp.zeros((HID,), jnp.float32), 'fc2_w': jax.random.normal(ks[5], (DIM, HID), jnp.float32) * s, 'fc2_b': jnp.zeros((DIM,), jnp.float32)}
    _L0_conv_all = _L0_conv_setup()
    _L0_conv_in = {k: v for k, v in _L0_conv_all.items() if k in ('qkv_w', 'qkv_b', 'proj_w', 'proj_b', 'rpb_table', 'norm1_g', 'norm1_b', 'norm2_g', 'norm2_b', 'fc1_w', 'fc1_b', 'fc2_w', 'fc2_b', )}
    del _L0_conv_all

    return {
        "x": x,
        "L0_conv_qkv_w": _L0_conv_in["qkv_w"],
        "L0_conv_qkv_b": _L0_conv_in["qkv_b"],
        "L0_conv_proj_w": _L0_conv_in["proj_w"],
        "L0_conv_proj_b": _L0_conv_in["proj_b"],
        "L0_conv_rpb_table": _L0_conv_in["rpb_table"],
        "L0_conv_norm1_g": _L0_conv_in["norm1_g"],
        "L0_conv_norm1_b": _L0_conv_in["norm1_b"],
        "L0_conv_norm2_g": _L0_conv_in["norm2_g"],
        "L0_conv_norm2_b": _L0_conv_in["norm2_b"],
        "L0_conv_fc1_w": _L0_conv_in["fc1_w"],
        "L0_conv_fc1_b": _L0_conv_in["fc1_b"],
        "L0_conv_fc2_w": _L0_conv_in["fc2_w"],
        "L0_conv_fc2_b": _L0_conv_in["fc2_b"],
    }

def reference(x, L0_conv_qkv_w, L0_conv_qkv_b, L0_conv_proj_w, L0_conv_proj_b, L0_conv_rpb_table, L0_conv_norm1_g, L0_conv_norm1_b, L0_conv_norm2_g, L0_conv_norm2_b, L0_conv_fc1_w, L0_conv_fc1_b, L0_conv_fc2_w, L0_conv_fc2_b):
    import jax
    import jax.numpy as jnp
    def _L0_conv_ref(x, qkv_w, qkv_b, proj_w, proj_b, rpb_table, norm1_g, norm1_b, norm2_g, norm2_b, fc1_w, fc1_b, fc2_w, fc2_b):
        import jax, jax.numpy as jnp
        import numpy as np
        DIM = 192
        HEADS = 6
        HD = DIM // HEADS
        WS = 7
        N = WS * WS
        SHIFT = 3
        HID = 768
        EPS = 1e-05
        SCALE = HD ** (-0.5)

        def _rel_pos_index():
            coords = np.stack(np.meshgrid(np.arange(WS), np.arange(WS), indexing='ij'))
            cf = coords.reshape(2, -1)
            rc = (cf[:, :, None] - cf[:, None, :]).transpose(1, 2, 0)
            rc[:, :, 0] += WS - 1
            rc[:, :, 1] += WS - 1
            rc[:, :, 0] *= 2 * WS - 1
            return rc.sum(-1)
        REL_IDX = jnp.asarray(_rel_pos_index().reshape(-1))

        def _attn_mask(H, W):
            img = np.zeros((H, W))
            sl = (slice(0, -WS), slice(-WS, -SHIFT), slice(-SHIFT, None))
            cnt = 0
            for hs in sl:
                for ws_ in sl:
                    img[hs, ws_] = cnt
                    cnt += 1
            m = img.reshape(H // WS, WS, W // WS, WS).transpose(0, 2, 1, 3).reshape(-1, N)
            diff = m[:, None, :] - m[:, :, None]
            return jnp.asarray(np.where(diff != 0, -100.0, 0.0).astype(np.float32))

        def _ln(x, g, b):
            mu = x.mean(-1, keepdims=True)
            var = ((x - mu) ** 2).mean(-1, keepdims=True)
            return (x - mu) * jax.lax.rsqrt(var + EPS) * g + b
        B, C, H, W = x.shape
        nW = H // WS * (W // WS)
        x = jnp.transpose(x, (0, 2, 3, 1))
        shortcut = x
        xn = _ln(x, norm1_g, norm1_b)
        xs = jnp.roll(xn, (-SHIFT, -SHIFT), axis=(1, 2))
        xw = xs.reshape(B, H // WS, WS, W // WS, WS, C).transpose(0, 1, 3, 2, 4, 5).reshape(-1, N, C)
        qkv = (xw @ qkv_w.T + qkv_b).reshape(-1, N, 3, HEADS, HD)
        q, k, v = (qkv[:, :, 0], qkv[:, :, 1], qkv[:, :, 2])
        attn = jnp.einsum('bnhd,bmhd->bhnm', q * SCALE, k)
        rpb = rpb_table[REL_IDX].reshape(N, N, HEADS).transpose(2, 0, 1)
        attn = attn + rpb[None]
        mask = _attn_mask(H, W)
        attn = attn.reshape(B, nW, HEADS, N, N) + mask[None, :, None]
        attn = jax.nn.softmax(attn.reshape(-1, HEADS, N, N), axis=-1)
        out = jnp.einsum('bhnm,bmhd->bnhd', attn, v).reshape(-1, N, C)
        out = out @ proj_w.T + proj_b
        out = out.reshape(B, H // WS, W // WS, WS, WS, C).transpose(0, 1, 3, 2, 4, 5).reshape(B, H, W, C)
        out = jnp.roll(out, (SHIFT, SHIFT), axis=(1, 2))
        x = shortcut + out
        h = _ln(x, norm2_g, norm2_b)
        h = jax.nn.gelu(h @ fc1_w.T + fc1_b, approximate=False)
        h = h @ fc2_w.T + fc2_b
        x = x + h
        return jnp.transpose(x, (0, 3, 1, 2))

    def _gn(v, G=32, eps=1e-5):
        B_, C_, H_, W_ = v.shape
        g = v.reshape(B_, G, C_ // G, H_, W_)
        m = jnp.mean(g, axis=(2, 3, 4), keepdims=True)
        s = jnp.var(g, axis=(2, 3, 4), keepdims=True)
        return ((g - m) / jnp.sqrt(s + eps)).reshape(v.shape)

    def _ln_c(v, eps=1e-6):
        m = jnp.mean(v, axis=1, keepdims=True)
        s = jnp.var(v, axis=1, keepdims=True)
        return (v - m) / jnp.sqrt(s + eps)

    def _ln_t(v, eps=1e-5):
        m = jnp.mean(v, axis=-1, keepdims=True)
        s = jnp.var(v, axis=-1, keepdims=True)
        return (v - m) / jnp.sqrt(s + eps)

    def _to_tokens(v):
        B_, C_, H_, W_ = v.shape
        return v.reshape(B_, C_, H_ * W_).transpose(0, 2, 1)
    def _from_tokens(t, like):
        B_, C_, H_, W_ = like.shape
        return t.transpose(0, 2, 1).reshape(B_, C_, H_, W_)

    x = _L0_conv_ref(x, L0_conv_qkv_w, L0_conv_qkv_b, L0_conv_proj_w, L0_conv_proj_b, L0_conv_rpb_table, L0_conv_norm1_g, L0_conv_norm1_b, L0_conv_norm2_g, L0_conv_norm2_b, L0_conv_fc1_w, L0_conv_fc1_b, L0_conv_fc2_w, L0_conv_fc2_b)
    return x


_drawn_inputs = setup_inputs


def setup_inputs(seed=0):
    import zlib

    import numpy as np

    out = dict(_drawn_inputs(seed))
    spreads = {'L0_conv_qkv_b': (0.0, 0.333),
     'L0_conv_proj_b': (0.0, 0.1),
     'L0_conv_norm1_g': (1.0, 0.6),
     'L0_conv_norm1_b': (0.0, 0.8),
     'L0_conv_norm2_g': (1.0, 0.6),
     'L0_conv_norm2_b': (0.0, 0.8),
     'L0_conv_fc1_b': (0.0, 0.1),
     'L0_conv_fc2_b': (0.0, 0.1)}
    factors = {'L0_conv_qkv_w': 3.784, 'L0_conv_rpb_table': 26.72}
    for name, (base, spread) in spreads.items():
        noise = np.random.default_rng([zlib.crc32(name.encode()), seed]).standard_normal(out[name].shape)
        drawn = base * np.exp(spread * noise) if base else spread * noise
        out[name] = jnp.asarray(drawn.astype(out[name].dtype))
    for name, factor in factors.items():
        out[name] = (out[name] * factor).astype(out[name].dtype)
    return out
```

```python
import concourse.bass as bass
from concourse import mybir
from contextlib import ExitStack

B, C, H, W = 16, 192, 56, 56
WS, SHIFT, HEADS, HID = 7, 3, 6, 768
EPS = 1e-5
HD = C // HEADS
N = WS * WS
NP = 64
NW = W // WS
NPAIR = NW // 2
T = WS * W
ROWS = H // WS
STRIPS = B * ROWS
PLAIN = B * (ROWS - 1)
CA, CB = 128, 64
PH = HEADS // 2
XG = T // 4
HT = HID // 128
QKV_SCALE, W_SCALE = 16.0, 64.0
SETUP_LOADS = 16 * 25
WIDE = 512
CUT = W - SHIFT


def swin_block(nc, x, w_qk, w_v, w_proj, w_fc1, w_fc2, b_qk, b_v, b_proj, b_fc1, b_fc2,
               g1, beta1, g2, beta2, rpb, mask, ident, out):
    f32, f16 = mybir.dt.float32, mybir.dt.float16
    ALU, ACT, AX = mybir.AluOpType, mybir.ActivationFunctionType, mybir.AxisListType
    ctx = ExitStack()
    with ctx:
        def sb(name, shape, dt=f32):
            return ctx.enter_context(nc.sbuf_tensor(name, shape, dt))

        def sem(name):
            return ctx.enter_context(nc.semaphore(name))

        ident_sb = sb("ident_sb", [128, 128])
        eps_sb = sb("eps_sb", [128, 4])
        power_sb = sb("power_sb", [128, 4])
        minus_sb = sb("minus_sb", [128, 4])
        g1_sb, beta1_sb = sb("g1_sb", [128, 2]), sb("beta1_sb", [128, 2])
        g2_sb, beta2_sb = sb("g2_sb", [128, 2]), sb("beta2_sb", [128, 2])
        stage_a = sb("stage_a", [128, 3 * C + HID + C])
        stage_b = sb("stage_b", [128, 3 * C + HID + C])
        stage_2 = sb("stage_2", [128, HT * C])
        NWT = 3 * C + HID + C
        OQK, OV, OF1, OPJ = 0, 2 * C, 3 * C, 3 * C + HID
        wa_hi, wa_lo = sb("wa_hi", [128, NWT], f16), sb("wa_lo", [128, NWT], f16)
        wb_hi, wb_lo = sb("wb_hi", [128, NWT], f16), sb("wb_lo", [128, NWT], f16)
        w2_hi, w2_lo = sb("w2_hi", [128, HT * C], f16), sb("w2_lo", [128, HT * C], f16)
        bias_in = sb("bias_in", [128, 5 + HT])
        bias = sb("bias", [128, 5 + HT])
        b_proj_sb = sb("b_proj_sb", [128, 2])
        b_fc2_sb = sb("b_fc2_sb", [128, 2])
        rpb_sb = sb("rpb_sb", [128, PH * N])
        mask_sb = sb("mask_sb", [128, 2, T])
        score_bias = sb("score_bias", [128, 2, PH, T])

        xa = [sb(f"xa{i}", [CA, T]) for i in range(2)]
        xb = [sb(f"xb{i}", [CB, T]) for i in range(2)]
        xw_a, xw_b = sb("xw_a", [CA, NW, NP]), sb("xw_b", [CB, NW, NP])
        stats1, mv1 = sb("stats1", [128, NPAIR, 6]), sb("mv1", [128, NPAIR, 2])
        var1, rstd1, shift1 = sb("var1", [128, 4]), sb("rstd1", [128, 4]), sb("shift1", [128, 4])
        xn_tok = sb("xn_tok", [128, NPAIR, C])
        xna_hi, xna_lo = sb("xna_hi", [CA, NW, NP], f16), sb("xna_lo", [CA, NW, NP], f16)
        xn3 = sb("xn3", [128, NW, NP], f16)
        q_hi, q_lo = sb("q_hi", [128, T], f16), sb("q_lo", [128, T], f16)
        k_hi, k_lo = sb("k_hi", [128, T], f16), sb("k_lo", [128, T], f16)
        q45_hi, q45_lo = sb("q45_hi", [64, T], f16), sb("q45_lo", [64, T], f16)
        k45_hi, k45_lo = sb("k45_hi", [64, T], f16), sb("k45_lo", [64, T], f16)
        v_hi, v_lo = sb("v_hi_sb", [128, NPAIR, C], f16), sb("v_lo_sb", [128, NPAIR, C], f16)
        logits = sb("logits", [128, PH, T])
        expd = sb("expd", [128, PH * NW, N])
        row_max, row_sum = sb("row_max", [128, PH * NW]), sb("row_sum", [128, PH * NW])
        row_inv = sb("row_inv", [128, PH * NW])
        probs = sb("probs", [128, PH, NW, NP])
        pt_hi_sb = sb("pt_hi_sb", [128, NPAIR, PH, 128], f16)
        pt_lo_sb = sb("pt_lo_sb", [128, NPAIR, PH, 128], f16)
        oa_hi, oa_lo = sb("oa_hi", [128, T], f16), sb("oa_lo", [128, T], f16)
        o3 = sb("o3", [128, T], f16)
        pj_a, pj_b = sb("pj_a", [CA, T]), sb("pj_b", [CB, T])
        x1_a, x1_b = sb("x1_a", [CA, T]), sb("x1_b", [CB, T])
        stats2, mv2 = sb("stats2", [128, 4, 6]), sb("mv2", [128, 4, 2])
        var2, rstd2, shift2 = sb("var2", [128, 4]), sb("rstd2", [128, 4]), sb("shift2", [128, 4])
        x2_tok = sb("x2_tok", [XG, 4, C])
        x2a_hi, x2a_lo = sb("x2a_hi", [CA, T], f16), sb("x2a_lo", [CA, T], f16)
        x23 = sb("x23", [128, T], f16)
        gelu = sb("gelu", [128, 2, T])
        h_hi, h_lo = sb("h_hi", [128, HT, T], f16), sb("h_lo", [128, HT, T], f16)
        f2_a, f2_b = sb("f2_a", [CA, T]), sb("f2_b", [CB, T])
        out_a, out_b = sb("out_a", [CA, T]), sb("out_b", [CB, T])

        ps_s = ctx.enter_context(nc.psum_tensor("ps_s", [128, PH, WIDE], f32))
        ps_o = ctx.enter_context(nc.psum_tensor("ps_o", [128, 2, WIDE], f32))
        ps_w = ctx.enter_context(nc.psum_tensor("ps_w", [128, 3, WIDE], f32))

        weights_in = sem("weights_in")
        bias_full = sem("bias_full")
        weights_ready = sem("weights_ready")
        dve_chain = sem("dve_chain")
        consts_ready = sem("consts_ready")
        x_loaded = [sem("x_loaded0"), sem("x_loaded1")]
        xw_ready = sem("xw_ready")
        xt_full = sem("xt_full")
        aggr1 = sem("aggr1")
        stat1_chain = sem("stat1_chain")
        pool_chain = sem("pool_chain")
        rstd1_ready = sem("rstd1_ready")
        norm1 = sem("norm1")
        nt_full = sem("nt_full")
        xn_hi, xn_lo = sem("xn_hi"), sem("xn_lo")
        qk_full = sem("qk_full")
        qk_hi, qk_lo = sem("qk_hi"), sem("qk_lo")
        v_full = sem("v_full")
        v_hi_done, v_lo_done = sem("v_hi_done"), sem("v_lo_done")
        s_full = sem("s_full")
        s_biased = sem("s_biased")
        s_max = sem("s_max")
        s_shifted = sem("s_shifted")
        p_exp = sem("p_exp")
        p_sum = sem("p_sum")
        p_inv = sem("p_inv")
        p_ready = sem("p_ready")
        pt_full = sem("pt_full")
        pt_hi, pt_lo = sem("pt_hi"), sem("pt_lo")
        o_full = sem("o_full")
        o_hi, o_lo = sem("o_hi"), sem("o_lo")
        pj_full = sem("pj_full")
        pj_out = sem("pj_out")
        x1_ready = sem("x1_ready")
        x1t_full = sem("x1t_full")
        stat2_chain = sem("stat2_chain")
        aggr2 = sem("aggr2")
        rstd2_ready = sem("rstd2_ready")
        norm2 = sem("norm2")
        n2_full = sem("n2_full")
        x2_hi, x2_lo = sem("x2_hi"), sem("x2_lo")
        f1_full = sem("f1_full")
        gelu_done = sem("gelu_done")
        hh_done = sem("hh_done")
        h_ready = sem("h_ready")
        f2_full = sem("f2_full")
        f2_out = sem("f2_out")
        out_ready = sem("out_ready")
        out_stored = sem("out_stored")

        passed_pe, passed_dve = sem("passed_pe"), sem("passed_dve")

        def wait(eng, semaphore, value):
            if not isinstance(value, int) or value > 0:
                eng.wait_ge(semaphore, value)

        def alone(eng, marks):
            eng.sem_inc(marks, 1)

        KINDS = [("pt", NPAIR, "back", (pt_hi, pt_lo)), ("nt", 2, "front", (xn_hi, xn_lo)),
                 ("pj", 2, "back", (pj_out,)), ("qk", 3, "front", (qk_hi, qk_lo)),
                 ("v", 2, "front", (v_hi_done, v_lo_done)), ("n2", 2, "back", (x2_hi, x2_lo)),
                 ("f1", HT, "back", (gelu_done,)), ("f2", 2, "back", (f2_out,))]
        JOBS = [(k, i, half, done, n) for k, n, half, done in KINDS for i in range(n)]
        PLACE = {(k, i): p for p, (k, i, *_) in enumerate(JOBS)}

        def bank(kind, i):
            return ps_w[:, PLACE[kind, i] % 3, :]

        def wait_bank(eng, kind, i, t, has_front, has_back):
            mine = PLACE[kind, i]
            before = [(p, 0) for p in range(mine - 3, -1, -3)]
            before += [(p, 1) for p in range(len(JOBS) - 1, -1, -1) if p % 3 == mine % 3]
            for p, ago in before:
                _, j, half, done, n = JOBS[p]
                if ago == 0 and not (has_front if half == "front" else has_back):
                    continue
                strip = t - ago - (half == "back")
                if ago:
                    j = n - 1
                for semaphore in done:
                    wait(eng, semaphore, (strip + 1) * n - (n - 1 - j))
                return

        block = ctx.enter_context(nc.Block())

        def dram_rows(tensor, b, c0, c1, row, rows):
            return tensor[bass.ds(b, 1), c0:c1, row * W:(row + rows) * W].rearrange("b c n -> (b c) n")

        def strip_parts(i):
            return [(WS * i + SHIFT, 4, 0), ((WS * i + SHIFT + 4) % H, 3, 4 * W)]

        @block.sync
        def _(sp):
            def load(b, i, slot):
                for row, rows, at in strip_parts(i):
                    sp.dma_start(xa[slot][:, at:at + rows * W],
                                 dram_rows(x, b, 0, CA, row, rows)).then_inc(x_loaded[slot], 16)
                    sp.dma_start(xb[slot][:, at:at + rows * W],
                                 dram_rows(x, b, CA, C, row, rows)).then_inc(x_loaded[slot], 16)

            def store(b, i):
                for row, rows, at in strip_parts(i):
                    sp.dma_start(dram_rows(out, b, 0, CA, row, rows),
                                 out_a[:, at:at + rows * W]).then_inc(out_stored, 16)
                    sp.dma_start(dram_rows(out, b, CA, C, row, rows),
                                 out_b[:, at:at + rows * W]).then_inc(out_stored, 16)

            def step(s, this, later, slot):
                if later is not None:
                    sp.wait_ge(x1_ready, s + 1)
                    load(*later, slot)
                sp.wait_ge(out_ready, s + 1)
                store(*this)

            load(0, 0, 0)
            load(0, 1, 1)
            per = ROWS - 1
            two = 2 * per

            def two_images(b, s):
                for k in range(two):
                    if k + 2 < two:
                        later = (b + (k + 2) // per, (k + 2) % per)
                    elif isinstance(b, int) and b + 2 >= B:
                        later = (k + 2 - two, ROWS - 1)
                    else:
                        later = (b + 2, k + 2 - two)
                    step(s + k, (b + k // per, k % per), later, k % 2)

            with sp.Fori(0, B // 2 - 1) as b2:
                two_images(b2 * 2, b2 * two)
            two_images(B - 2, PLAIN - two)
            with sp.Fori(0, B // 2 - 1) as b2:
                for k in range(2):
                    step(b2 * 2 + (PLAIN + k), (b2 * 2 + k, ROWS - 1),
                         (b2 * 2 + (k + 2), ROWS - 1), k)
            for k in range(2):
                step(STRIPS - 2 + k, (B - 2 + k, ROWS - 1), None, k)
            sp.wait_ge(out_stored, 64 * STRIPS)

        @block.tensor
        def _(pe):
            def five(dst, lhs_rhs):
                for n, (lhs, rhs) in enumerate(lhs_rhs):
                    last = nc.tensor.matmul(dst, lhs, rhs, start=n == 0, stop=n == 4)
                return last

            def weights_moving(dst, a_hi, a_lo, three, col, n):
                cols = slice(col, col + n)
                return five(dst, [(a_hi, wa_hi[:, cols]), (a_hi, wa_lo[:, cols]),
                                  (a_lo, wa_hi[:, cols]), (three, wb_hi[:, cols]),
                                  (three, wb_lo[:, cols])])

            def weights_still(dst, a_hi, a_lo, three, col, n):
                cols = slice(col, col + n)
                return five(dst, [(wa_hi[:, cols], a_hi), (wa_hi[:, cols], a_lo),
                                  (wa_lo[:, cols], a_hi), (wb_hi[:, cols], three),
                                  (wb_lo[:, cols], three)])

            pe.wait_ge(weights_in, SETUP_LOADS)
            cols = [(OQK, 128, beta1_sb), (OQK + 128, 128, beta1_sb), (OQK + 256, 128, beta1_sb),
                    (OV, 128, beta1_sb), (OV + 128, 64, beta1_sb)]
            cols += [(OF1 + 128 * j, 128, beta2_sb) for j in range(HT)]
            for n, (col, m, beta) in enumerate(cols):
                nc.tensor.matmul(ps_w[0:m, 0, n:n + 1], stage_a[:, col:col + m], beta[:, 0:1],
                                 start=True, stop=False)
                last = nc.tensor.matmul(ps_w[0:m, 0, n:n + 1], stage_b[0:CB, col:col + m],
                                        beta[0:CB, 1:2], start=False, stop=True)
            last.then_inc(bias_full, 1)
            pe.wait_ge(weights_ready, 1)

            def to_tokens_1(t):
                pe.wait_ge(xw_ready, t + 1)
                wait(pe, s_biased, t)
                for g in range(NPAIR):
                    dst = ps_s[:, g // 2, (g % 2) * C:(g % 2 + 1) * C]
                    nc.tensor.transpose(dst[:, 0:CA], xw_a[:, 2 * g:2 * g + 2, :], ident_sb[:, :])
                    last = nc.tensor.transpose(dst[:, CA:C], xw_b[:, 2 * g:2 * g + 2, :],
                                               ident_sb[0:CB, 0:CB])
                    if g % 2:
                        last.then_inc(xt_full, 1)

            def to_channels_1(t, **has):
                pe.wait_ge(norm1, 4 * t + 4)
                for i in range(2):
                    wait_bank(pe, "nt", i, t, **has)
                    alone(pe, passed_pe)
                    for g in range(NPAIR):
                        c0, m = ((0, CA), (CA, CB))[i]
                        last = nc.tensor.transpose(bank("nt", i)[0:m, 128 * g:128 * g + 128],
                                                   xn_tok[:, g, c0:c0 + m], ident_sb[:, :])
                    last.then_inc(nt_full, 1)

            def queries_keys(t, **has):
                pe.wait_ge(xn_hi, 2 * t + 2)
                pe.wait_ge(xn_lo, 2 * t + 2)
                for i in range(3):
                    wait_bank(pe, "qk", i, t, **has)
                    dst = bank("qk", i)[:, 0:T].rearrange("p (w n) -> p w n", n=N)
                    weights_still(dst, xna_hi[:, :, 0:N], xna_lo[:, :, 0:N], xn3[:, :, 0:N],
                                  OQK + 128 * i, 128).then_inc(qk_full, 1)

            def values(t, **has):
                for i in range(2):
                    wait_bank(pe, "v", i, t, **has)
                    for g in (2 * i, 2 * i + 1):
                        pair = slice(2 * g, 2 * g + 2)
                        last = weights_moving(bank("v", i)[:, (g % 2) * C:(g % 2 + 1) * C],
                                              xna_hi[:, pair, :], xna_lo[:, pair, :],
                                              xn3[:, pair, :], OV, C)
                    last.then_inc(v_full, 1)

            def scores(t):
                pe.wait_ge(qk_hi, 3 * t + 3)
                pe.wait_ge(qk_lo, 3 * t + 3)
                for w in range(NW):
                    win = slice(w * N, w * N + N)
                    for n in range(3):
                        for h in range(HEADS):
                            qh, ql, kh, kl = (q_hi, q_lo, k_hi, k_lo) if h < 4 else \
                                (q45_hi, q45_lo, k45_hi, k45_lo)
                            rows = slice(HD * (h % 4), HD * (h % 4) + HD)
                            lhs, rhs = ((qh, kh), (qh, kl), (ql, kh))[n]
                            par = NP * (h % 2)
                            last = nc.tensor.matmul(ps_s[par:par + N, h // 2, win], lhs[rows, win],
                                                    rhs[rows, win], start=n == 0, stop=n == 2,
                                                    skip_group_check=True)
                last.then_inc(s_full, 1)

            def turn_probs(u, **has):
                pe.wait_ge(p_ready, u + 1)
                for g in range(NPAIR):
                    wait_bank(pe, "pt", g, u + 1, **has)
                    for p in range(PH):
                        last = nc.tensor.transpose(bank("pt", g)[:, 128 * p:128 * p + 128],
                                                   probs[:, p, 2 * g:2 * g + 2, :], ident_sb[:, :])
                    last.then_inc(pt_full, 1)

            def attend(u):
                pe.wait_ge(v_hi_done, 2 * u + 2)
                pe.wait_ge(v_lo_done, 2 * u + 2)
                for g in range(NPAIR):
                    pe.wait_ge(pt_hi, 4 * u + g + 1)
                    pe.wait_ge(pt_lo, 4 * u + g + 1)
                    alone(pe, passed_pe)
                    for heads in (range(4), range(4, HEADS)):
                        for n in range(3):
                            vs, ps = ((v_hi, pt_hi_sb), (v_hi, pt_lo_sb), (v_lo, pt_hi_sb))[n]
                            for odd in range(2):
                                rows = slice(NP * odd, NP * odd + N)
                                for h in heads:
                                    col = (T // 2) * (h // 4) + g * N
                                    par = NP * (h % 2)
                                    last = nc.tensor.matmul(
                                        ps_o[HD * (h % 4):HD * (h % 4) + HD, odd, col:col + N],
                                        vs[rows, g, HD * h:HD * h + HD],
                                        ps[rows, g, h // 2, par:par + N],
                                        start=n == 0, stop=n == 2, skip_group_check=True)
                last.then_inc(o_full, 1)

            def project(u, **has):
                pe.wait_ge(o_hi, 2 * u + 2)
                pe.wait_ge(o_lo, 2 * u + 2)
                for i, m in ((0, CA), (1, CB)):
                    wait_bank(pe, "pj", i, u + 1, **has)
                    weights_still(bank("pj", i)[0:m, 0:T], oa_hi[:, :], oa_lo[:, :], o3[:, :],
                                  OPJ + CA * i, m).then_inc(pj_full, 1)

            def to_tokens_2(u):
                pe.wait_ge(x1_ready, u + 1)
                for g in range(4):
                    dst = ps_o[0:XG, g // 2, (g % 2) * C:(g % 2 + 1) * C]
                    cols = slice(XG * g, XG * g + XG)
                    nc.tensor.transpose(dst[:, 0:CA], x1_a[:, cols], ident_sb[:, :])
                    last = nc.tensor.transpose(dst[:, CA:C], x1_b[:, cols], ident_sb[0:CB, 0:CB])
                    if g % 2:
                        last.then_inc(x1t_full, 1)

            def to_channels_2(u, **has):
                pe.wait_ge(norm2, 4 * u + 4)
                for i in range(2):
                    wait_bank(pe, "n2", i, u + 1, **has)
                    alone(pe, passed_pe)
                    for g in range(4):
                        c0, m = ((0, CA), (CA, CB))[i]
                        last = nc.tensor.transpose(bank("n2", i)[0:m, XG * g:XG * g + XG],
                                                   x2_tok[:, g, c0:c0 + m], ident_sb[0:XG, 0:XG])
                    last.then_inc(n2_full, 1)

            def hidden(u, **has):
                pe.wait_ge(x2_hi, 2 * u + 2)
                pe.wait_ge(x2_lo, 2 * u + 2)
                for j in range(HT):
                    wait_bank(pe, "f1", j, u + 1, **has)
                    weights_still(bank("f1", j)[:, 0:T], x2a_hi[:, :], x2a_lo[:, :], x23[:, :],
                                  OF1 + 128 * j, 128).then_inc(f1_full, 1)

            def contract(u, **has):
                for i in range(2):
                    wait_bank(pe, "f2", i, u + 1, **has)
                for j in range(HT):
                    pe.wait_ge(h_ready, HT * u + j + 1)
                    for i, m in ((0, CA), (1, CB)):
                        cols = slice(C * j + CA * i, C * j + CA * i + m)
                        for n, (w2, hh) in enumerate(((w2_hi, h_hi), (w2_hi, h_lo), (w2_lo, h_hi))):
                            last = nc.tensor.matmul(bank("f2", i)[0:m, 0:T], w2[:, cols], hh[:, j, :],
                                                    start=j == 0 and n == 0,
                                                    stop=j == HT - 1 and n == 2)
                        if j == HT - 1:
                            last.then_inc(f2_full, 1)

            def iteration(t, front=True, back=True):
                u = t - 1
                has = {"has_front": front, "has_back": back}
                if front:
                    to_tokens_1(t)
                if back:
                    turn_probs(u, **has)
                    attend(u)
                if front:
                    to_channels_1(t, **has)
                if back:
                    project(u, **has)
                if front:
                    queries_keys(t, **has)
                    values(t, **has)
                if back:
                    to_tokens_2(u)
                if front:
                    scores(t)
                if back:
                    to_channels_2(u, **has)
                    hidden(u, **has)
                    contract(u, **has)

            iteration(0, back=False)
            iteration(1)
            with pe.Fori(2, STRIPS) as t:
                iteration(t)
            iteration(STRIPS, front=False)

        @block.scalar
        def _(act):
            ID = ACT.Identity

            act.dma_start(stage_a[:, OQK:OV], w_qk[0:CA, :]).then_inc(weights_in, 16)
            act.dma_start(stage_a[:, OV:OF1], w_v[0:CA, :]).then_inc(weights_in, 16)
            act.dma_start(stage_a[:, OF1:OPJ], w_fc1[0:CA, :]).then_inc(weights_in, 16)
            act.dma_start(stage_a[:, OPJ:NWT], w_proj[0:CA, :]).then_inc(weights_in, 16)
            for half in range(2):
                rows = slice(CB * half, CB * half + CB)
                act.dma_start(stage_b[rows, OQK:OV], w_qk[CA:C, :]).then_inc(weights_in, 16)
                act.dma_start(stage_b[rows, OV:OF1], w_v[CA:C, :]).then_inc(weights_in, 16)
                act.dma_start(stage_b[rows, OF1:OPJ], w_fc1[CA:C, :]).then_inc(weights_in, 16)
                act.dma_start(stage_b[rows, OPJ:NWT], w_proj[CA:C, :]).then_inc(weights_in, 16)
            act.dma_start(stage_2[:, :], w_fc2).then_inc(weights_in, 16)
            for dst, src in ((g1_sb, g1), (beta1_sb, beta1), (g2_sb, g2), (beta2_sb, beta2),
                             (b_proj_sb, b_proj), (b_fc2_sb, b_fc2), (rpb_sb, rpb),
                             (ident_sb, ident)):
                act.dma_start(dst[:, :], src).then_inc(weights_in, 16)
            act.dma_start(mask_sb[:, :, :], mask).then_inc(weights_in, 16)
            act.dma_start(bias_in[:, 0:3], b_qk).then_inc(weights_in, 16)
            act.dma_start(bias_in[:, 3:5], b_v).then_inc(weights_in, 16)
            act.dma_start(bias_in[:, 5:5 + HT], b_fc1).then_inc(weights_in, 16)
            act.wait_ge(weights_ready, 1)

            def normalise_1(t):
                act.wait_ge(rstd1_ready, t + 1)
                for g in range(NPAIR):
                    act.activation(xn_tok[:, g, :], ps_s[:, g // 2, (g % 2) * C:(g % 2 + 1) * C], ID,
                                   bias=shift1[:, g:g + 1], scale=rstd1[:, g:g + 1]).then_inc(norm1, 1)

            def probs_hi(u):
                for g in range(NPAIR):
                    act.wait_ge(pt_full, 4 * u + g + 1)
                    act.copy(pt_hi_sb[:, g, :, :], bank("pt", g)[:, 0:PH * 128]
                             .rearrange("p (a n) -> p a n", a=PH)).then_inc(pt_hi, 1)

            def attended_hi(u):
                act.wait_ge(o_full, u + 1)
                act.activation(oa_hi[:, :].rearrange("p (b n) -> p b n", b=2), ps_o[:, :, 0:T // 2], ID,
                               bias=bias[:, 3:4]).then_inc(o_hi, 1)
                act.activation(o3[0:CB, :].rearrange("p (b n) -> p b n", b=2),
                               ps_o[0:CB, :, T // 2:T], ID, bias=bias[0:CB, 4:5]).then_inc(o_hi, 1)

            def normed_hi_1(t):
                for i, m, dst in ((0, CA, xna_hi), (1, CB, xn3)):
                    act.wait_ge(nt_full, 2 * t + i + 1)
                    act.copy(dst[0:m, :, :], bank("nt", i)[0:m, :].rearrange("p (w n) -> p w n", w=NW)
                             ).then_inc(xn_hi, 1)

            def projected(u):
                for i, m, dst in ((0, CA, pj_a), (1, CB, pj_b)):
                    act.wait_ge(pj_full, 2 * u + i + 1)
                    wait(act, x1_ready, u)
                    rolled = dst[:, :].rearrange("p (r w b c) -> p b w r c", r=WS, b=2, c=WS)
                    src = bank("pj", i)[0:m, 0:T].rearrange("p (b w r c) -> p b w r c", b=2,
                                                            r=WS, c=WS)
                    for odd in range(2):
                        last = act.activation(rolled[:, odd], src[:, odd], ID,
                                              bias=b_proj_sb[0:m, i:i + 1],
                                              scale=1.0 / (QKV_SCALE * W_SCALE))
                    last.then_inc(pj_out, 1)

            def queries_keys_hi(t):
                for i, dst in ((0, q_hi), (1, k_hi)):
                    act.wait_ge(qk_full, 3 * t + i + 1)
                    act.activation(dst[:, :], bank("qk", i)[:, 0:T], ID,
                                   bias=bias[:, i:i + 1]).then_inc(qk_hi, 1)
                act.wait_ge(qk_full, 3 * t + 3)
                act.activation(q45_hi[:, :], bank("qk", 2)[0:64, 0:T], ID, bias=bias[0:64, 2:3])
                act.activation(k45_hi[:, :], bank("qk", 2)[64:128, 0:T], ID,
                               bias=bias[64:128, 2:3]).then_inc(qk_hi, 1)

            def values_hi(t):
                for i in range(2):
                    act.wait_ge(v_full, 2 * t + i + 1)
                    act.copy(v_hi[:, 2 * i:2 * i + 2, :], bank("v", i)[:, 0:2 * C]
                             .rearrange("p (g c) -> p g c", g=2)).then_inc(v_hi_done, 1)

            def normalise_2(u):
                act.wait_ge(rstd2_ready, u + 1)
                for g in range(4):
                    act.activation(x2_tok[:, g, :], ps_o[0:XG, g // 2, (g % 2) * C:(g % 2 + 1) * C],
                                   ID, bias=shift2[0:XG, g:g + 1],
                                   scale=rstd2[0:XG, g:g + 1]).then_inc(norm2, 1)

            def normed_hi_2(u):
                for i, m, dst in ((0, CA, x2a_hi), (1, CB, x23)):
                    act.wait_ge(n2_full, 2 * u + i + 1)
                    act.copy(dst[0:m, :], bank("n2", i)[0:m, 0:T]).then_inc(x2_hi, 1)

            def activate(u):
                for j in range(HT):
                    act.wait_ge(f1_full, HT * u + j + 1)
                    wait(act, h_ready, HT * u + j - 1 if j > 1 else HT * u)
                    act.activation(gelu[:, j % 2, :], bank("f1", j)[:, 0:T], ACT.Gelu,
                                   bias=bias[:, 5 + j:6 + j], scale=1.0 / W_SCALE
                                   ).then_inc(gelu_done, 1)

            def exponent(t):
                act.wait_ge(s_shifted, t + 1)
                wait(act, p_ready, t)
                act.activation(expd[:, :, :].rearrange("p a n -> p (a n)"),
                               logits[:, :, :].rearrange("p a n -> p (a n)"), ACT.Exp
                               ).then_inc(p_exp, 1)

            def contracted(u):
                for i, m, dst in ((0, CA, f2_a), (1, CB, f2_b)):
                    act.wait_ge(f2_full, 2 * u + i + 1)
                    wait(act, out_ready, u)
                    act.activation(dst[:, :], bank("f2", i)[0:m, 0:T], ID,
                                   bias=b_fc2_sb[0:m, i:i + 1], scale=1.0 / W_SCALE
                                   ).then_inc(f2_out, 1)

            def iteration(t, front=True, back=True):
                u = t - 1
                if front:
                    normalise_1(t)
                if back:
                    probs_hi(u)
                    attended_hi(u)
                if front:
                    normed_hi_1(t)
                if back:
                    projected(u)
                if front:
                    queries_keys_hi(t)
                    values_hi(t)
                if back:
                    normalise_2(u)
                    normed_hi_2(u)
                    activate(u)
                if front:
                    exponent(t)
                if back:
                    contracted(u)

            iteration(0, back=False)
            iteration(1)
            with act.Fori(2, STRIPS) as t:
                iteration(t)
            iteration(STRIPS, front=False)

        @block.vector
        def _(dve):
            links = [0]

            def link(instruction):
                links[0] += 1
                instruction.then_inc(dve_chain, 1)
                dve.wait_ge(dve_chain, links[0])

            dve.memset(ps_s[:, :, :], 0.0)
            dve.memset(xw_a[:, :, :], 0.0)
            dve.memset(xw_b[:, :, :], 0.0)
            dve.wait_ge(weights_in, SETUP_LOADS)
            for kind in range(2):
                for p in range(PH):
                    dve.tensor_tensor(
                        score_bias[:, kind, p, :].rearrange("p (w n) -> p w n", n=N),
                        mask_sb[:, kind, :].rearrange("p (w n) -> p w n", n=N),
                        rpb_sb[:, N * p:N * p + N].unsqueeze(1).to_broadcast([128, NW, N]), ALU.add)
            dve.wait_ge(bias_full, 1)
            for rows, lo, hi, scale in ((128, 0, 4, QKV_SCALE), (64, 4, 5, QKV_SCALE),
                                        (128, 5, 5 + HT, 1.0)):
                link(dve.tensor_tensor(bias[0:rows, lo:hi], ps_w[0:rows, 0, lo:hi],
                                       bias_in[0:rows, lo:hi], ALU.add))
                link(dve.tensor_scalar(bias[0:rows, lo:hi], bias[0:rows, lo:hi], scale, None,
                                       ALU.mult))
            for stage, hi_t, lo_t, part in ((stage_a, wa_hi, wa_lo, 0), (stage_b, wb_hi, wb_lo, 1)):
                for c0, c1, gain, scale in ((OQK, OF1, g1_sb, QKV_SCALE), (OF1, OPJ, g2_sb, W_SCALE),
                                            (OPJ, NWT, None, W_SCALE)):
                    s = stage[:, c0:c1]
                    if gain is None:
                        link(dve.tensor_scalar(s, s, scale, None, ALU.mult))
                    else:
                        link(dve.tensor_scalar(s, s, gain[:, part:part + 1], scale, ALU.mult,
                                               ALU.mult))
                    link(dve.tensor_copy(hi_t[:, c0:c1], s))
                    dve.tensor_tensor(lo_t[:, c0:c1], s, hi_t[:, c0:c1], ALU.subtract)
            link(dve.tensor_scalar(stage_2[:, :], stage_2[:, :], W_SCALE, None, ALU.mult))
            link(dve.tensor_copy(w2_hi[:, :], stage_2[:, :]))
            dve.tensor_tensor(w2_lo[:, :], stage_2[:, :], w2_hi[:, :], ALU.subtract
                              ).then_inc(weights_ready, 1)

            def to_windows(t, slot, count):
                dve.wait_ge(x_loaded[slot], count)
                wait(dve, xt_full, 2 * t)
                for src, dst in ((xa[slot], xw_a), (xb[slot], xw_b)):
                    rows = src[:, :].rearrange("p (r c) -> p r c", r=WS)
                    wins = dst[:, :, 0:N].rearrange("p w (r c) -> p w r c", r=WS)
                    dve.tensor_copy(wins[:, 0:NW - 1], rows[:, :, SHIFT:SHIFT + T // WS - WS]
                                    .rearrange("p r (w c) -> p w r c", c=WS))
                    dve.tensor_copy(wins[:, NW - 1, :, 0:WS - SHIFT], rows[:, :, W - WS + SHIFT:W])
                    last = dve.tensor_copy(wins[:, NW - 1, :, WS - SHIFT:WS], rows[:, :, 0:SHIFT])
                last.then_inc(xw_ready, 1)

            def statistics(rows, full, t, banks, stats, mv, chain, done):
                for g in range(4):
                    if g % 2 == 0:
                        dve.wait_ge(full, 2 * t + g // 2 + 1)
                    last = dve.bn_stats(stats[0:rows, g, :],
                                        banks[0:rows, g // 2, (g % 2) * C:(g % 2 + 1) * C])
                last.then_inc(chain, 1)
                dve.wait_ge(chain, t + 1)
                alone(dve, passed_dve)
                for g in range(4):
                    last = dve.bn_aggr(mv[0:rows, g, :], stats[0:rows, g, :])
                last.then_inc(done, 1)

            def probs_lo(u):
                for g in range(NPAIR):
                    dve.wait_ge(pt_hi, 4 * u + g + 1)
                    dve.tensor_tensor(pt_lo_sb[:, g, :, :], bank("pt", g)[:, 0:PH * 128]
                                      .rearrange("p (a n) -> p a n", a=PH), pt_hi_sb[:, g, :, :],
                                      ALU.subtract).then_inc(pt_lo, 1)

            def attended_lo(u):
                dve.wait_ge(o_hi, 2 * u + 2)
                dve.scalar_tensor_tensor(oa_lo[:, :].rearrange("p (b n) -> p b n", b=2),
                                         ps_o[:, :, 0:T // 2], bias[:, 3:4],
                                         oa_hi[:, :].rearrange("p (b n) -> p b n", b=2),
                                         ALU.add, ALU.subtract).then_inc(o_lo, 1)
                dve.scalar_tensor_tensor(o3[CB:128, :].rearrange("p (b n) -> p b n", b=2),
                                         ps_o[0:CB, :, T // 2:T], bias[0:CB, 4:5],
                                         o3[0:CB, :].rearrange("p (b n) -> p b n", b=2),
                                         ALU.add, ALU.subtract).then_inc(o_lo, 1)

            def normed_lo_1(t):
                dve.wait_ge(xn_hi, 2 * t + 1)
                dve.tensor_tensor(xna_lo[:, :, :], bank("nt", 0).rearrange("p (w n) -> p w n", w=NW),
                                  xna_hi[:, :, :], ALU.subtract).then_inc(xn_lo, 1)
                dve.wait_ge(xn_hi, 2 * t + 2)
                dve.tensor_tensor(xn3[CB:128, :, :],
                                  bank("nt", 1)[0:CB, :].rearrange("p (w n) -> p w n", w=NW),
                                  xn3[0:CB, :, :], ALU.subtract).then_inc(xn_lo, 1)

            def queries_keys_lo(t):
                for i, hi, lo in ((0, q_hi, q_lo), (1, k_hi, k_lo)):
                    dve.wait_ge(qk_hi, 3 * t + i + 1)
                    dve.scalar_tensor_tensor(lo[:, :], bank("qk", i)[:, 0:T], bias[:, i:i + 1],
                                             hi[:, :], ALU.add, ALU.subtract).then_inc(qk_lo, 1)
                dve.wait_ge(qk_hi, 3 * t + 3)
                dve.scalar_tensor_tensor(q45_lo[:, :], bank("qk", 2)[0:64, 0:T], bias[0:64, 2:3],
                                         q45_hi[:, :], ALU.add, ALU.subtract)
                dve.scalar_tensor_tensor(k45_lo[:, :], bank("qk", 2)[64:128, 0:T],
                                         bias[64:128, 2:3], k45_hi[:, :], ALU.add,
                                         ALU.subtract).then_inc(qk_lo, 1)

            def values_lo(t):
                for i in range(2):
                    dve.wait_ge(v_hi_done, 2 * t + i + 1)
                    dve.tensor_tensor(v_lo[:, 2 * i:2 * i + 2, :], bank("v", i)[:, 0:2 * C]
                                      .rearrange("p (g c) -> p g c", g=2),
                                      v_hi[:, 2 * i:2 * i + 2, :], ALU.subtract
                                      ).then_inc(v_lo_done, 1)

            def normed_lo_2(u):
                dve.wait_ge(x2_hi, 2 * u + 1)
                dve.tensor_tensor(x2a_lo[:, :], bank("n2", 0)[:, 0:T], x2a_hi[:, :],
                                  ALU.subtract).then_inc(x2_lo, 1)
                dve.wait_ge(x2_hi, 2 * u + 2)
                dve.tensor_tensor(x23[CB:128, :], bank("n2", 1)[0:CB, 0:T], x23[0:CB, :],
                                  ALU.subtract).then_inc(x2_lo, 1)

            def logits_and_max(t, kind):
                dve.wait_ge(s_full, t + 1)
                wait(dve, p_exp, t)
                dve.scalar_tensor_tensor(logits[:, :, :], ps_s[:, :, 0:T],
                                         HD ** -0.5 / (QKV_SCALE * QKV_SCALE),
                                         score_bias[:, kind, :, :], ALU.mult, ALU.add
                                         ).then_inc(s_biased, 1)
                dve.wait_ge(s_biased, t + 1)
                dve.tensor_reduce(row_max[:, :], logits[:, :, :].rearrange("p a (w n) -> p (a w) n", n=N),
                                  AX.X, ALU.max).then_inc(s_max, 1)

            def split_hidden(u):
                for j in range(HT):
                    dve.wait_ge(gelu_done, HT * u + j + 1)
                    dve.tensor_copy(h_hi[:, j, :], gelu[:, j % 2, :]).then_inc(hh_done, 1)
                    dve.wait_ge(hh_done, HT * u + j + 1)
                    dve.tensor_tensor(h_lo[:, j, :], gelu[:, j % 2, :], h_hi[:, j, :],
                                      ALU.subtract).then_inc(h_ready, 1)

            def row_sums(t):
                dve.wait_ge(p_exp, t + 1)
                dve.tensor_reduce(row_sum[:, :], expd[:, :, :], AX.X, ALU.add).then_inc(p_sum, 1)
                dve.wait_ge(p_sum, t + 1)
                dve.reciprocal(row_inv[:, :], row_sum[:, :]).then_inc(p_inv, 1)

            def iteration(t, slot, kind, front=True, back=True, following=True, count=None):
                u = t - 1
                if front:
                    statistics(128, xt_full, t, ps_s, stats1, mv1, stat1_chain, aggr1)
                if back:
                    probs_lo(u)
                    attended_lo(u)
                if front:
                    normed_lo_1(t)
                    queries_keys_lo(t)
                    values_lo(t)
                if back:
                    statistics(XG, x1t_full, u, ps_o, stats2, mv2, stat2_chain, aggr2)
                    normed_lo_2(u)
                if front:
                    logits_and_max(t, kind)
                if back:
                    split_hidden(u)
                if front:
                    row_sums(t)
                if following:
                    to_windows(t + 1, 1 - slot, count)

            to_windows(0, 0, 64)
            def pairs(t, kind):
                iteration(t, 0, kind, count=32 * t + 64)
                iteration(t + 1, 1, kind, count=32 * t + 128)

            iteration(0, 0, 0, back=False, count=64)
            iteration(1, 1, 0, count=128)
            with dve.Fori(2, PLAIN, 2) as t:
                pairs(t, 0)
            with dve.Fori(PLAIN, STRIPS - 2, 2) as t:
                pairs(t, 1)
            iteration(STRIPS - 2, 0, 1, count=32 * STRIPS)
            iteration(STRIPS - 1, 1, 1, following=False)
            iteration(STRIPS, 0, 1, front=False, following=False)

        @block.gpsimd
        def _(pool):
            pool.memset(eps_sb[:, :], EPS)
            pool.memset(power_sb[:, :], -0.5)
            pool.memset(minus_sb[:, :], -1.0)
            pool.memset(probs[:, :, :, :], 0.0).then_inc(consts_ready, 1)
            pool.wait_ge(consts_ready, 1)

            def inverse_deviation(rows, t, aggr, mv, var, rstd, shift, chain, ready):
                pool.wait_ge(aggr, t + 1)
                pool.tensor_tensor(var[0:rows, :], mv[0:rows, :, 1], eps_sb[0:rows, :], ALU.add)
                pool.tensor_tensor(shift[0:rows, :], mv[0:rows, :, 0], minus_sb[0:rows, :],
                                   ALU.mult).then_inc(pool_chain, 1)
                pool.wait_ge(pool_chain, chain + 1)
                pool.tensor_tensor(rstd[0:rows, :], var[0:rows, :], power_sb[0:rows, :],
                                   ALU.pow).then_inc(pool_chain, 1)
                pool.wait_ge(pool_chain, chain + 2)
                pool.tensor_tensor(shift[0:rows, :], shift[0:rows, :], rstd[0:rows, :],
                                   ALU.mult).then_inc(ready, 1)

            def residual(u, slot):
                wait(pool, out_ready, u)
                pool.wait_ge(pj_out, 2 * u + 2)
                for pj, xs, x1 in ((pj_a, xa[slot], x1_a), (pj_b, xb[slot], x1_b)):
                    pj_r, x_r, x1_r = (a[:, :].rearrange("p (r c) -> p r c", r=WS)
                                       for a in (pj, xs, x1))
                    pool.tensor_tensor(x1_r[:, :, SHIFT:W], pj_r[:, :, 0:CUT], x_r[:, :, SHIFT:W],
                                       ALU.add)
                    last = pool.tensor_tensor(x1_r[:, :, 0:SHIFT], pj_r[:, :, CUT:W],
                                              x_r[:, :, 0:SHIFT], ALU.add)
                last.then_inc(x1_ready, 1)

            def subtract_max(t):
                pool.wait_ge(s_max, t + 1)
                rows = logits[:, :, :].rearrange("p a (w n) -> p (a w) n", n=N)
                pool.tensor_tensor(rows, rows, row_max[:, :].unsqueeze(2)
                                   .to_broadcast([128, PH * NW, N]), ALU.subtract
                                   ).then_inc(s_shifted, 1)

            def normalise(t):
                pool.wait_ge(p_inv, t + 1)
                wait(pool, pt_full, 4 * t)
                pool.tensor_tensor(probs[:, :, :, 0:N].rearrange("p a w n -> p (a w) n"),
                                   expd[:, :, :], row_inv[:, :].unsqueeze(2)
                                   .to_broadcast([128, PH * NW, N]), ALU.mult
                                   ).then_inc(p_ready, 1)

            def finish(u):
                pool.wait_ge(f2_out, 2 * u + 2)
                wait(pool, out_stored, 64 * u)
                pool.tensor_tensor(out_a[:, :], f2_a[:, :], x1_a[:, :], ALU.add)
                pool.tensor_tensor(out_b[:, :], f2_b[:, :], x1_b[:, :], ALU.add
                                   ).then_inc(out_ready, 1)

            def iteration(t, slot, front=True, back=True, chain=0):
                u = t - 1
                if front:
                    inverse_deviation(128, t, aggr1, mv1, var1, rstd1, shift1, chain, rstd1_ready)
                    chain = chain + 2
                if back:
                    residual(u, 1 - slot)
                    inverse_deviation(XG, u, aggr2, mv2, var2, rstd2, shift2, chain, rstd2_ready)
                if front:
                    subtract_max(t)
                    normalise(t)
                if back:
                    finish(u)

            iteration(0, 0, back=False)
            iteration(1, 1, chain=2)
            with pool.Fori(2, STRIPS, 2) as t:
                iteration(t, 0, chain=4 * t - 2)
                iteration(t + 1, 1, chain=4 * t + 2)
            iteration(STRIPS, 0, front=False, chain=4 * STRIPS - 2)


def kernel(x, L0_conv_qkv_w, L0_conv_qkv_b, L0_conv_proj_w, L0_conv_proj_b, L0_conv_rpb_table,
           L0_conv_norm1_g, L0_conv_norm1_b, L0_conv_norm2_g, L0_conv_norm2_b,
           L0_conv_fc1_w, L0_conv_fc1_b, L0_conv_fc2_w, L0_conv_fc2_b):
    import numpy as np
    import concourse.bacc as bacc
    from concourse.bass_utils import run_bass_kernel_spmd as run

    def lay(a):
        return np.ascontiguousarray(a)

    x = np.asarray(x)
    qkv_w, qkv_b = np.asarray(L0_conv_qkv_w), np.asarray(L0_conv_qkv_b)

    def two_columns(v):
        v = np.asarray(v)
        return lay(np.stack([v[:CA], np.concatenate([v[CA:], v[CA:]])], axis=1))

    order = np.concatenate([np.arange(0, CA), np.arange(C, C + CA),
                            np.arange(CA, C), np.arange(C + CA, 2 * C)])
    r, c = np.divmod(np.arange(N), WS)
    index = (r[:, None] - r[None, :] + WS - 1) * (2 * WS - 1) + (c[:, None] - c[None, :] + WS - 1)
    gathered = np.asarray(L0_conv_rpb_table)[index]
    rpb = np.zeros((128, PH, N), np.float32)
    for h in range(HEADS):
        rpb[NP * (h % 2):NP * (h % 2) + N, h // 2] = gathered[:, :, h]
    late_r, late_c = r >= WS - SHIFT, c >= WS - SHIFT
    mask = np.zeros((128, 2, NW, N), np.float32)
    for kind in range(2):
        for w in range(NW):
            apart = np.zeros((N, N), bool)
            if kind == 1:
                apart |= late_r[:, None] != late_r[None, :]
            if w == NW - 1:
                apart |= late_c[:, None] != late_c[None, :]
            for half in (0, NP):
                mask[half:half + N, kind, w] = np.where(apart, np.float32(-100), np.float32(0))

    fc2_t = np.asarray(L0_conv_fc2_w).T
    arrays = {
        "x": lay(x.reshape(B, C, H * W)),
        "w_qk": lay(qkv_w[order].T),
        "w_v": lay(qkv_w[2 * C:].T),
        "w_proj": lay(np.asarray(L0_conv_proj_w).T),
        "w_fc1": lay(np.asarray(L0_conv_fc1_w).T),
        "w_fc2": lay(fc2_t.reshape(HT, 128, C).transpose(1, 0, 2).reshape(128, HT * C)),
        "b_qk": lay(qkv_b[order].reshape(3, 128).T),
        "b_v": two_columns(qkv_b[2 * C:]),
        "b_proj": two_columns(L0_conv_proj_b),
        "b_fc1": lay(np.asarray(L0_conv_fc1_b).reshape(HT, 128).T),
        "b_fc2": two_columns(L0_conv_fc2_b),
        "g1": two_columns(L0_conv_norm1_g),
        "beta1": two_columns(L0_conv_norm1_b),
        "g2": two_columns(L0_conv_norm2_g),
        "beta2": two_columns(L0_conv_norm2_b),
        "rpb": lay(rpb.reshape(128, PH * N)),
        "mask": lay(mask.reshape(128, 2, T)),
        "ident": np.eye(128, dtype=np.float32),
    }
    nc = bacc.Bacc("TRN2", target_bir_lowering=False, num_devices=1)
    args = [nc.dram_tensor(f"in_{k}", a.shape, mybir.dt.from_np(a.dtype), kind="ExternalInput").ap()
            for k, a in arrays.items()]
    result = nc.dram_tensor("out_dram", (B, C, H * W), mybir.dt.float32, kind="ExternalOutput").ap()
    swin_block(nc, *args, result)
    r = run(nc, [{f"in_{k}": a for k, a in arrays.items()}], core_ids=[0])
    return r.results[0]["out_dram"].reshape(B, C, H, W)
```

```python
import concourse.bass as bass
from concourse import mybir
from contextlib import ExitStack

B, C, H, W = 16, 192, 56, 56
WS, SHIFT, HEADS, HID = 7, 3, 6, 768
EPS = 1e-5
HD = C // HEADS
N = WS * WS
NP = 64
NW = W // WS
NPAIR = NW // 2
T = WS * W
ROWS = H // WS
STRIPS = B * ROWS
PLAIN = B * (ROWS - 1)
CA, CB = 128, 64
PH = HEADS // 2
XG = T // 4
HT = HID // 128
QKV_SCALE, W_SCALE = 16.0, 64.0
SETUP_LOADS = 16 * 25
WIDE = 512
CUT = W - SHIFT


def swin_block(nc, x, w_qk, w_v, w_proj, w_fc1, w_fc2, b_qk, b_v, b_proj, b_fc1, b_fc2,
               g1, beta1, g2, beta2, rpb, mask, ident, out):
    f32, f16 = mybir.dt.float32, mybir.dt.float16
    ALU, ACT, AX = mybir.AluOpType, mybir.ActivationFunctionType, mybir.AxisListType
    ctx = ExitStack()
    with ctx:
        def sb(name, shape, dt=f32):
            return ctx.enter_context(nc.sbuf_tensor(name, shape, dt))

        def sem(name):
            return ctx.enter_context(nc.semaphore(name))

        ident_sb = sb("ident_sb", [128, 128])
        eps_sb = sb("eps_sb", [128, 4])
        power_sb = sb("power_sb", [128, 4])
        minus_sb = sb("minus_sb", [128, 4])
        g1_sb, beta1_sb = sb("g1_sb", [128, 2]), sb("beta1_sb", [128, 2])
        g2_sb, beta2_sb = sb("g2_sb", [128, 2]), sb("beta2_sb", [128, 2])
        stage_a = sb("stage_a", [128, 3 * C + HID + C])
        stage_b = sb("stage_b", [128, 3 * C + HID + C])
        stage_2 = sb("stage_2", [128, HT * C])
        NWT = 3 * C + HID + C
        OQK, OV, OF1, OPJ = 0, 2 * C, 3 * C, 3 * C + HID
        wa_hi, wa_lo = sb("wa_hi", [128, NWT], f16), sb("wa_lo", [128, NWT], f16)
        wb_hi, wb_lo = sb("wb_hi", [128, NWT], f16), sb("wb_lo", [128, NWT], f16)
        w2_hi, w2_lo = sb("w2_hi", [128, HT * C], f16), sb("w2_lo", [128, HT * C], f16)
        w2_both = sb("w2_both", [128, HT, 128], f16)
        bias_in = sb("bias_in", [128, 5 + HT])
        bias = sb("bias", [128, 5 + HT])
        b_proj_sb = sb("b_proj_sb", [128, 2])
        b_fc2_sb = sb("b_fc2_sb", [128, 2])
        rpb_sb = sb("rpb_sb", [128, PH * N])
        mask_sb = sb("mask_sb", [128, 2, T])
        score_bias = sb("score_bias", [128, 2, PH, T])

        xa = [sb(f"xa{i}", [CA, T]) for i in range(2)]
        xb = [sb(f"xb{i}", [CB, T]) for i in range(2)]
        xw_a, xw_b = sb("xw_a", [CA, NW, NP]), sb("xw_b", [CB, NW, NP])
        stats1, mv1 = sb("stats1", [128, NPAIR, 6]), sb("mv1", [128, NPAIR, 2])
        var1, rstd1, shift1 = sb("var1", [128, 4]), sb("rstd1", [128, 4]), sb("shift1", [128, 4])
        xn_tok = sb("xn_tok", [128, NPAIR, C])
        xna_hi, xna_lo = sb("xna_hi", [CA, NW, NP], f16), sb("xna_lo", [CA, NW, NP], f16)
        xn3 = sb("xn3", [128, NW, NP], f16)
        q_hi, q_lo = sb("q_hi", [128, T], f16), sb("q_lo", [128, T], f16)
        k_hi, k_lo = sb("k_hi", [128, T], f16), sb("k_lo", [128, T], f16)
        q45_hi, q45_lo = sb("q45_hi", [64, T], f16), sb("q45_lo", [64, T], f16)
        k45_hi, k45_lo = sb("k45_hi", [64, T], f16), sb("k45_lo", [64, T], f16)
        v_hi, v_lo = sb("v_hi_sb", [128, NPAIR, C], f16), sb("v_lo_sb", [128, NPAIR, C], f16)
        logits = sb("logits", [128, PH, T])
        expd = sb("expd", [128, PH, T])
        row_max, row_sum = sb("row_max", [128, PH, NW]), sb("row_sum", [128, PH, NW])
        row_inv = sb("row_inv", [128, PH, NW])
        probs = sb("probs", [128, PH, NW, NP])
        pt_hi_sb = sb("pt_hi_sb", [128, NPAIR, PH, 128], f16)
        pt_lo_sb = sb("pt_lo_sb", [128, NPAIR, PH, 128], f16)
        oa_hi, oa_lo = sb("oa_hi", [128, T], f16), sb("oa_lo", [128, T], f16)
        o3 = sb("o3", [128, T], f16)
        pj_a, pj_b = sb("pj_a", [CA, T]), sb("pj_b", [CB, T])
        x1_a = [sb(f"x1_a{i}", [CA, T]) for i in range(2)]
        x1_b = [sb(f"x1_b{i}", [CB, T]) for i in range(2)]
        stats2, mv2 = sb("stats2", [128, 4, 6]), sb("mv2", [128, 4, 2])
        var2, rstd2, shift2 = sb("var2", [128, 4]), sb("rstd2", [128, 4]), sb("shift2", [128, 4])
        x2_tok = sb("x2_tok", [XG, 4, C])
        x2a_hi, x2a_lo = sb("x2a_hi", [CA, T], f16), sb("x2a_lo", [CA, T], f16)
        x23 = sb("x23", [128, T], f16)
        warm = sb("warm", [1, 2])
        gelu = sb("gelu", [128, 3, T])
        h_hi, h_lo = sb("h_hi", [128, HT, T], f16), sb("h_lo", [128, HT, T], f16)
        f2_a, f2_b = sb("f2_a", [CA, T]), sb("f2_b", [CB, T])
        out_a, out_b = sb("out_a", [CA, T]), sb("out_b", [CB, T])

        ps_s = ctx.enter_context(nc.psum_tensor("ps_s", [128, PH, WIDE], f32))
        ps_o = ctx.enter_context(nc.psum_tensor("ps_o", [128, 2, WIDE], f32))
        ps_w = ctx.enter_context(nc.psum_tensor("ps_w", [128, 3, WIDE], f32))

        weights_in = sem("weights_in")
        bias_full = sem("bias_full")
        weights_ready = sem("weights_ready")
        dve_chain = sem("dve_chain")
        consts_ready = sem("consts_ready")
        x_loaded = [sem("x_loaded0"), sem("x_loaded1")]
        xw_ready = sem("xw_ready")
        xt_full = sem("xt_full")
        aggr1 = sem("aggr1")
        stat1_chain = sem("stat1_chain")
        pool_chain = sem("pool_chain")
        rstd1_ready = sem("rstd1_ready")
        norm1 = sem("norm1")
        nt_full = sem("nt_full")
        xn_hi, xn_lo = sem("xn_hi"), sem("xn_lo")
        qk_full = sem("qk_full")
        qk_hi, qk_lo = sem("qk_hi"), sem("qk_lo")
        v_full = sem("v_full")
        v_hi_done, v_lo_done = sem("v_hi_done"), sem("v_lo_done")
        s_full = sem("s_full")
        s_biased = sem("s_biased")
        s_max = sem("s_max")
        s_shifted = sem("s_shifted")
        p_exp = sem("p_exp")
        p_sum = sem("p_sum")
        p_inv = sem("p_inv")
        p_ready = sem("p_ready")
        pt_full = sem("pt_full")
        pt_hi, pt_lo = sem("pt_hi"), sem("pt_lo")
        o_full = sem("o_full")
        o_hi, o_lo = sem("o_hi"), sem("o_lo")
        pj_full = sem("pj_full")
        pj_out = sem("pj_out")
        x1_ready = sem("x1_ready")
        x1t_full = sem("x1t_full")
        stat2_chain = sem("stat2_chain")
        aggr2 = sem("aggr2")
        rstd2_ready = sem("rstd2_ready")
        norm2 = sem("norm2")
        n2_full = sem("n2_full")
        x2_hi, x2_lo = sem("x2_hi"), sem("x2_lo")
        f1_full = sem("f1_full")
        gelu_done = sem("gelu_done")
        hh_done = sem("hh_done")
        h_ready = sem("h_ready")
        f2_full = sem("f2_full")
        f2_half = sem("f2_half")
        f2_sum = sem("f2_sum")
        out_ready = sem("out_ready")
        out_stored = sem("out_stored")

        passed_pe, passed_dve = sem("passed_pe"), sem("passed_dve")

        def wait(eng, semaphore, value):
            if not isinstance(value, int) or value > 0:
                eng.wait_ge(semaphore, value)

        def alone(eng, marks):
            eng.sem_inc(marks, 1)

        KINDS = [("pt", 0, NPAIR, 1, (pt_hi, pt_lo), NPAIR), ("f1", 3, 2, 2, (gelu_done,), HT),
                 ("nt", 0, 2, 0, (xn_hi, xn_lo), 2), ("f1", 5, 1, 2, (gelu_done,), HT),
                 ("pj", 0, 2, 1, (pj_out,), 2), ("qk", 0, 3, 0, (qk_hi, qk_lo), 3),
                 ("v", 0, 2, 0, (v_hi_done, v_lo_done), 2), ("f2", 0, 2, 2, (f2_sum,), 2)]
        JOBS = [(k, first + i, lag, done, per) for k, first, n, lag, done, per in KINDS
                for i in range(n)]
        PLACE = {(k, i): p for p, (k, i, *_) in enumerate(JOBS)}
        assert len(JOBS) % 3 == 0

        def bank(kind, i):
            if kind == "f1" and i < 3:
                return ps_s[:, i, :]
            if kind == "n2":
                return ps_o[:, i, :]
            return ps_w[:, PLACE[kind, i] % 3, :]

        def wait_bank(eng, kind, i, t, stages):
            mine = PLACE[kind, i]
            before = [(p, 0) for p in range(mine - 3, -1, -3)]
            before += [(p, 1) for p in range(len(JOBS) - 1, -1, -1) if p % 3 == mine % 3]
            for p, ago in before:
                _, j, lag, done, per = JOBS[p]
                if ago == 0 and lag not in stages:
                    continue
                for semaphore in done:
                    wait(eng, semaphore, (t - ago - lag) * per + j + 1)
                return

        block = ctx.enter_context(nc.Block())

        def dram_rows(tensor, b, c0, c1, row, rows):
            return tensor[bass.ds(b, 1), c0:c1, row * W:(row + rows) * W].rearrange("b c n -> (b c) n")

        def strip_parts(i):
            return [(WS * i + SHIFT, 4, 0), ((WS * i + SHIFT + 4) % H, 3, 4 * W)]

        @block.sync
        def _(sp):
            def load(b, i, slot):
                for row, rows, at in strip_parts(i):
                    sp.dma_start(xa[slot][:, at:at + rows * W],
                                 dram_rows(x, b, 0, CA, row, rows)).then_inc(x_loaded[slot], 16)
                    sp.dma_start(xb[slot][:, at:at + rows * W],
                                 dram_rows(x, b, CA, C, row, rows)).then_inc(x_loaded[slot], 16)

            def store(b, i):
                for row, rows, at in strip_parts(i):
                    sp.dma_start(dram_rows(out, b, 0, CA, row, rows),
                                 out_a[:, at:at + rows * W]).then_inc(out_stored, 16)
                    sp.dma_start(dram_rows(out, b, CA, C, row, rows),
                                 out_b[:, at:at + rows * W]).then_inc(out_stored, 16)

            def step(s, this, later, slot):
                if later is not None:
                    sp.wait_ge(x1_ready, s + 2)
                    load(*later, slot)
                sp.wait_ge(out_ready, s + 1)
                store(*this)

            load(0, 0, 0)
            load(0, 1, 1)
            sp.wait_ge(x1_ready, 1)
            load(0, 2, 0)
            per = ROWS - 1
            two = 2 * per

            def two_images(b, s):
                for k in range(two):
                    if k + 3 < two:
                        later = (b + (k + 3) // per, (k + 3) % per)
                    elif isinstance(b, int) and b + 2 >= B:
                        later = (k + 3 - two, ROWS - 1)
                    else:
                        later = (b + 2, k + 3 - two)
                    step(s + k, (b + k // per, k % per), later, (k + 1) % 2)

            with sp.Fori(0, B // 2 - 1) as b2:
                two_images(b2 * 2, b2 * two)
            two_images(B - 2, PLAIN - two)
            with sp.Fori(0, B // 2 - 2) as b2:
                for k in range(2):
                    step(b2 * 2 + (PLAIN + k), (b2 * 2 + k, ROWS - 1),
                         (b2 * 2 + (k + 3), ROWS - 1), (k + 1) % 2)
            for b in range(B - 4, B):
                later = (b + 3, ROWS - 1) if b + 3 < B else None
                step(PLAIN + b, (b, ROWS - 1), later, (b + 1) % 2)
            sp.wait_ge(out_stored, 64 * STRIPS)

        @block.tensor
        def _(pe):
            def five(dst, lhs_rhs):
                for n, (lhs, rhs) in enumerate(lhs_rhs):
                    last = nc.tensor.matmul(dst, lhs, rhs, start=n == 0, stop=n == 4)
                return last

            def weights_moving(dst, a_hi, a_lo, three, col, n):
                cols = slice(col, col + n)
                return five(dst, [(a_hi, wa_hi[:, cols]), (a_hi, wa_lo[:, cols]),
                                  (a_lo, wa_hi[:, cols]), (three, wb_hi[:, cols]),
                                  (three, wb_lo[:, cols])])

            def weights_still(dst, a_hi, a_lo, three, col, n):
                cols = slice(col, col + n)
                return five(dst, [(wa_hi[:, cols], a_hi), (wa_hi[:, cols], a_lo),
                                  (wa_lo[:, cols], a_hi), (wb_hi[:, cols], three),
                                  (wb_lo[:, cols], three)])

            pe.wait_ge(weights_in, SETUP_LOADS)
            cols = [(OQK, 128, beta1_sb), (OQK + 128, 128, beta1_sb), (OQK + 256, 128, beta1_sb),
                    (OV, 128, beta1_sb), (OV + 128, 64, beta1_sb)]
            cols += [(OF1 + 128 * j, 128, beta2_sb) for j in range(HT)]
            for n, (col, m, beta) in enumerate(cols):
                nc.tensor.matmul(ps_w[0:m, 0, n:n + 1], stage_a[:, col:col + m], beta[:, 0:1],
                                 start=True, stop=False)
                last = nc.tensor.matmul(ps_w[0:m, 0, n:n + 1], stage_b[0:CB, col:col + m],
                                        beta[0:CB, 1:2], start=False, stop=True)
            last.then_inc(bias_full, 1)
            pe.wait_ge(weights_ready, 1)

            def to_tokens_1(t):
                pe.wait_ge(xw_ready, t + 1)
                wait(pe, s_biased, PH * t)
                wait(pe, gelu_done, HT * (t - 2) + 2)
                for g in range(NPAIR):
                    dst = ps_s[:, g // 2, (g % 2) * C:(g % 2 + 1) * C]
                    nc.tensor.transpose(dst[:, 0:CA], xw_a[:, 2 * g:2 * g + 2, :], ident_sb[:, :])
                    last = nc.tensor.transpose(dst[:, CA:C], xw_b[:, 2 * g:2 * g + 2, :],
                                               ident_sb[0:CB, 0:CB])
                    if g % 2:
                        last.then_inc(xt_full, 1)

            def to_channels_1(t, stages):
                pe.wait_ge(norm1, 4 * t + 4)
                for i in range(2):
                    wait_bank(pe, "nt", i, t, stages)
                    alone(pe, passed_pe)
                    for g in range(NPAIR):
                        c0, m = ((0, CA), (CA, CB))[i]
                        last = nc.tensor.transpose(bank("nt", i)[0:m, 128 * g:128 * g + 128],
                                                   xn_tok[:, g, c0:c0 + m], ident_sb[:, :])
                    last.then_inc(nt_full, 1)

            def queries_keys(t, stages):
                pe.wait_ge(xn_hi, 2 * t + 2)
                pe.wait_ge(xn_lo, 2 * t + 2)
                for i in range(3):
                    wait_bank(pe, "qk", i, t, stages)
                    dst = bank("qk", i)[:, 0:T].rearrange("p (w n) -> p w n", n=N)
                    weights_still(dst, xna_hi[:, :, 0:N], xna_lo[:, :, 0:N], xn3[:, :, 0:N],
                                  OQK + 128 * i, 128).then_inc(qk_full, 1)

            def values(t, i, stages):
                wait_bank(pe, "v", i, t, stages)
                for g in (2 * i, 2 * i + 1):
                    pair = slice(2 * g, 2 * g + 2)
                    last = weights_moving(bank("v", i)[:, (g % 2) * C:(g % 2 + 1) * C],
                                          xna_hi[:, pair, :], xna_lo[:, pair, :],
                                          xn3[:, pair, :], OV, C)
                last.then_inc(v_full, 1)

            def scores(t, p):
                done = 3 if p == PH - 1 else 2
                pe.wait_ge(qk_hi, 3 * t + done)
                pe.wait_ge(qk_lo, 3 * t + done)
                wait(pe, gelu_done, HT * (t - 2) + 3)
                qh, ql, kh, kl = (q_hi, q_lo, k_hi, k_lo) if p < 2 else \
                    (q45_hi, q45_lo, k45_hi, k45_lo)
                for w in range(NW):
                    win = slice(w * N, w * N + N)
                    for n in range(3):
                        for par in range(2):
                            r = HD * ((2 * p + par) % 4)
                            lhs, rhs = ((qh, kh), (qh, kl), (ql, kh))[n]
                            last = nc.tensor.matmul(ps_s[NP * par:NP * par + N, p, win],
                                                    lhs[r:r + HD, win], rhs[r:r + HD, win],
                                                    start=n == 0, stop=n == 2,
                                                    skip_group_check=True)
                last.then_inc(s_full, 1)

            def turn_probs(u, stages):
                pe.wait_ge(p_ready, PH * u + PH)
                for g in range(NPAIR):
                    wait_bank(pe, "pt", g, u + 1, stages)
                    for p in range(PH):
                        last = nc.tensor.transpose(bank("pt", g)[:, 128 * p:128 * p + 128],
                                                   probs[:, p, 2 * g:2 * g + 2, :], ident_sb[:, :])
                    last.then_inc(pt_full, 1)

            def attend(u, pairs):
                pe.wait_ge(v_hi_done, 2 * u + 2)
                pe.wait_ge(v_lo_done, 2 * u + 2)
                for g in pairs:
                    pe.wait_ge(pt_hi, 4 * u + g + 1)
                    pe.wait_ge(pt_lo, 4 * u + g + 1)
                    alone(pe, passed_pe)
                    for heads in (range(4), range(4, HEADS)):
                        for n in range(3):
                            vs, ps = ((v_hi, pt_hi_sb), (v_hi, pt_lo_sb), (v_lo, pt_hi_sb))[n]
                            for odd in range(2):
                                rows = slice(NP * odd, NP * odd + N)
                                for h in heads:
                                    col = (T // 2) * (h // 4) + g * N
                                    par = NP * (h % 2)
                                    last = nc.tensor.matmul(
                                        ps_o[HD * (h % 4):HD * (h % 4) + HD, odd, col:col + N],
                                        vs[rows, g, HD * h:HD * h + HD],
                                        ps[rows, g, h // 2, par:par + N],
                                        start=n == 0, stop=n == 2, skip_group_check=True)
                if g == NPAIR - 1:
                    last.then_inc(o_full, 1)

            def project(u, stages):
                pe.wait_ge(o_hi, 2 * u + 2)
                pe.wait_ge(o_lo, 2 * u + 2)
                for i, m in ((0, CA), (1, CB)):
                    wait_bank(pe, "pj", i, u + 1, stages)
                    weights_still(bank("pj", i)[0:m, 0:T], oa_hi[:, :], oa_lo[:, :], o3[:, :],
                                  OPJ + CA * i, m).then_inc(pj_full, 1)

            def to_tokens_2(u, slot):
                pe.wait_ge(x1_ready, u + 1)
                for g in range(4):
                    dst = ps_o[0:XG, g // 2, (g % 2) * C:(g % 2 + 1) * C]
                    cols = slice(XG * g, XG * g + XG)
                    nc.tensor.transpose(dst[:, 0:CA], x1_a[slot][:, cols], ident_sb[:, :])
                    last = nc.tensor.transpose(dst[:, CA:C], x1_b[slot][:, cols],
                                               ident_sb[0:CB, 0:CB])
                    if g % 2:
                        last.then_inc(x1t_full, 1)

            def to_channels_2(u):
                pe.wait_ge(norm2, 4 * u + 4)
                alone(pe, passed_pe)
                for i in range(2):
                    for g in range(4):
                        c0, m = ((0, CA), (CA, CB))[i]
                        last = nc.tensor.transpose(bank("n2", i)[0:m, XG * g:XG * g + XG],
                                                   x2_tok[:, g, c0:c0 + m], ident_sb[0:XG, 0:XG])
                    last.then_inc(n2_full, 1)

            def hidden_first(u, stages):
                pe.wait_ge(x2_hi, 2 * u + 2)
                pe.wait_ge(x2_lo, 2 * u + 2)
                if 0 in stages:
                    pe.wait_ge(s_biased, PH * (u + 2))
                for j in range(3):
                    hidden_item(j)

            def hidden_item(j):
                weights_still(bank("f1", j)[:, 0:T], x2a_hi[:, :], x2a_lo[:, :], x23[:, :],
                              OF1 + 128 * j, 128).then_inc(f1_full, 1)

            def hidden_rest(m, items, stages):
                for j in items:
                    wait_bank(pe, "f1", j, m + 2, stages)
                    hidden_item(j)

            def contract(m, items, stages):
                if 0 in items:
                    for i in range(2):
                        wait_bank(pe, "f2", i, m + 2, stages)
                for j in items:
                    pe.wait_ge(h_ready, HT * m + j + 1)
                    cols = slice(C * j, C * j + CA)
                    for n, (w2, hh) in enumerate(((w2_hi, h_hi), (w2_hi, h_lo), (w2_lo, h_hi))):
                        last = nc.tensor.matmul(bank("f2", 0)[:, 0:T], w2[:, cols], hh[:, j, :],
                                                start=j == 0 and n == 0,
                                                stop=j == HT - 1 and n == 2)
                    if j == HT - 1:
                        last.then_inc(f2_full, 1)
                    for n, hh in enumerate((h_hi, h_lo)):
                        last = nc.tensor.matmul(bank("f2", 1)[:, 0:T], w2_both[:, j, :], hh[:, j, :],
                                                start=j == 0 and n == 0,
                                                stop=j == HT - 1 and n == 1)
                    if j == HT - 1:
                        last.then_inc(f2_full, 1)

            def iteration(t, slot, stages=(0, 1, 2)):
                front, back, mlp = (n in stages for n in range(3))
                u, m = t - 1, t - 2
                if front:
                    to_tokens_1(t)
                if back:
                    turn_probs(u, stages)
                for half in range(2):
                    if mlp:
                        hidden_rest(m, (3 + half,), stages)
                    if back:
                        attend(u, (2 * half, 2 * half + 1))
                if front:
                    to_channels_1(t, stages)
                if mlp:
                    hidden_rest(m, (5,), stages)
                if back:
                    project(u, stages)
                if front:
                    queries_keys(t, stages)
                    scores(t, 0)
                    values(t, 0, stages)
                if back:
                    to_tokens_2(u, 1 - slot)
                if front:
                    scores(t, 1)
                    values(t, 1, stages)
                    scores(t, 2)
                if mlp:
                    contract(m, range(4), stages)
                if back:
                    to_channels_2(u)
                if mlp:
                    contract(m, range(4, HT), stages)
                if back:
                    hidden_first(u, stages)

            iteration(0, 0, (0,))
            iteration(1, 1, (0, 1))
            iteration(2, 0)
            iteration(3, 1)
            with pe.Fori(4, STRIPS, 2) as t:
                iteration(t, 0)
                iteration(t + 1, 1)
            iteration(STRIPS, 0, (1, 2))
            iteration(STRIPS + 1, 1, (2,))

        @block.scalar
        def _(act):
            ID = ACT.Identity

            act.dma_start(stage_a[:, OQK:OV], w_qk[0:CA, :]).then_inc(weights_in, 16)
            act.dma_start(stage_a[:, OV:OF1], w_v[0:CA, :]).then_inc(weights_in, 16)
            act.dma_start(stage_a[:, OF1:OPJ], w_fc1[0:CA, :]).then_inc(weights_in, 16)
            act.dma_start(stage_a[:, OPJ:NWT], w_proj[0:CA, :]).then_inc(weights_in, 16)
            for half in range(2):
                rows = slice(CB * half, CB * half + CB)
                act.dma_start(stage_b[rows, OQK:OV], w_qk[CA:C, :]).then_inc(weights_in, 16)
                act.dma_start(stage_b[rows, OV:OF1], w_v[CA:C, :]).then_inc(weights_in, 16)
                act.dma_start(stage_b[rows, OF1:OPJ], w_fc1[CA:C, :]).then_inc(weights_in, 16)
                act.dma_start(stage_b[rows, OPJ:NWT], w_proj[CA:C, :]).then_inc(weights_in, 16)
            act.dma_start(stage_2[:, :], w_fc2).then_inc(weights_in, 16)
            for dst, src in ((g1_sb, g1), (beta1_sb, beta1), (g2_sb, g2), (beta2_sb, beta2),
                             (b_proj_sb, b_proj), (b_fc2_sb, b_fc2), (rpb_sb, rpb),
                             (ident_sb, ident)):
                act.dma_start(dst[:, :], src).then_inc(weights_in, 16)
            act.dma_start(mask_sb[:, :, :], mask).then_inc(weights_in, 16)
            act.dma_start(bias_in[:, 0:3], b_qk).then_inc(weights_in, 16)
            act.dma_start(bias_in[:, 3:5], b_v).then_inc(weights_in, 16)
            act.dma_start(bias_in[:, 5:5 + HT], b_fc1).then_inc(weights_in, 16)
            act.wait_ge(weights_ready, 1)
            act.wait_ge(consts_ready, 1)

            def normalise_1(t):
                act.wait_ge(rstd1_ready, t + 1)
                for g in range(NPAIR):
                    act.activation(xn_tok[:, g, :], ps_s[:, g // 2, (g % 2) * C:(g % 2 + 1) * C], ID,
                                   bias=shift1[:, g:g + 1], scale=rstd1[:, g:g + 1]).then_inc(norm1, 1)

            def probs_hi(u):
                for g in range(NPAIR):
                    act.wait_ge(pt_full, 4 * u + g + 1)
                    act.copy(pt_hi_sb[:, g, :, :], bank("pt", g)[:, 0:PH * 128]
                             .rearrange("p (a n) -> p a n", a=PH)).then_inc(pt_hi, 1)

            def attended_hi(u):
                act.wait_ge(o_full, u + 1)
                act.activation(oa_hi[:, :].rearrange("p (b n) -> p b n", b=2), ps_o[:, :, 0:T // 2], ID,
                               bias=bias[:, 3:4]).then_inc(o_hi, 1)
                act.activation(o3[0:CB, :].rearrange("p (b n) -> p b n", b=2),
                               ps_o[0:CB, :, T // 2:T], ID, bias=bias[0:CB, 4:5]).then_inc(o_hi, 1)

            def normed_hi_1(t):
                for i, m, dst in ((0, CA, xna_hi), (1, CB, xn3)):
                    act.wait_ge(nt_full, 2 * t + i + 1)
                    act.copy(dst[0:m, :, :], bank("nt", i)[0:m, :].rearrange("p (w n) -> p w n", w=NW)
                             ).then_inc(xn_hi, 1)

            def projected(u):
                for i, m, dst in ((0, CA, pj_a), (1, CB, pj_b)):
                    act.wait_ge(pj_full, 2 * u + i + 1)
                    wait(act, x1_ready, u)
                    rolled = dst[:, :].rearrange("p (r w b c) -> p b w r c", r=WS, b=2, c=WS)
                    src = bank("pj", i)[0:m, 0:T].rearrange("p (b w r c) -> p b w r c", b=2,
                                                            r=WS, c=WS)
                    for odd in range(2):
                        last = act.activation(rolled[:, odd], src[:, odd], ID,
                                              bias=b_proj_sb[0:m, i:i + 1],
                                              scale=1.0 / (QKV_SCALE * W_SCALE))
                    last.then_inc(pj_out, 1)

            def queries_keys_hi(t):
                for i, dst in ((0, q_hi), (1, k_hi)):
                    act.wait_ge(qk_full, 3 * t + i + 1)
                    act.activation(dst[:, :], bank("qk", i)[:, 0:T], ID,
                                   bias=bias[:, i:i + 1]).then_inc(qk_hi, 1)
                act.wait_ge(qk_full, 3 * t + 3)
                act.activation(q45_hi[:, :], bank("qk", 2)[0:64, 0:T], ID, bias=bias[0:64, 2:3])
                act.activation(k45_hi[:, :], bank("qk", 2)[64:128, 0:T], ID,
                               bias=bias[64:128, 2:3]).then_inc(qk_hi, 1)

            def values_hi(t, i):
                act.wait_ge(v_full, 2 * t + i + 1)
                act.copy(v_hi[:, 2 * i:2 * i + 2, :], bank("v", i)[:, 0:2 * C]
                         .rearrange("p (g c) -> p g c", g=2)).then_inc(v_hi_done, 1)

            def normalise_2(u):
                act.wait_ge(rstd2_ready, u + 1)
                for g in range(4):
                    act.activation(x2_tok[:, g, :], ps_o[0:XG, g // 2, (g % 2) * C:(g % 2 + 1) * C],
                                   ID, bias=shift2[0:XG, g:g + 1],
                                   scale=rstd2[0:XG, g:g + 1]).then_inc(norm2, 1)

            def normed_hi_2(u):
                for i, m, dst in ((0, CA, x2a_hi), (1, CB, x23)):
                    act.wait_ge(n2_full, 2 * u + i + 1)
                    act.copy(dst[0:m, :], bank("n2", i)[0:m, 0:T]).then_inc(x2_hi, 1)

            def activate(s, items):
                for j in items:
                    act.wait_ge(f1_full, HT * s + j + 1)
                    wait(act, h_ready, HT * s + j - 2)
                    act.activation(gelu[:, j % 3, :], bank("f1", j)[:, 0:T], ACT.Gelu,
                                   bias=bias[:, 5 + j:6 + j], scale=1.0 / W_SCALE
                                   ).then_inc(gelu_done, 1)

            def exponent(t, p):
                act.wait_ge(s_shifted, PH * t + p + 1)
                wait(act, p_ready, PH * (t - 1) + p + 1)
                act.activation(expd[:, p, :], logits[:, p, :], ACT.Exp).then_inc(p_exp, 1)

            def iteration(t, stages=(0, 1, 2)):
                front, back, mlp = (n in stages for n in range(3))
                u, m = t - 1, t - 2
                if back:
                    probs_hi(u)
                if front:
                    normalise_1(t)
                if mlp:
                    activate(m, (3, 4))
                if back:
                    attended_hi(u)
                if front:
                    normed_hi_1(t)
                if mlp:
                    activate(m, (5,))
                if back:
                    projected(u)
                if front:
                    queries_keys_hi(t)
                    values_hi(t, 0)
                    exponent(t, 0)
                    values_hi(t, 1)
                    exponent(t, 1)
                if back:
                    normalise_2(u)
                if front:
                    exponent(t, 2)
                if back:
                    normed_hi_2(u)
                    act.activation(warm[:, 1:2], warm[:, 0:1], ACT.Gelu)
                    activate(u, (0, 1, 2))

            iteration(0, (0,))
            iteration(1, (0, 1))
            iteration(2)
            iteration(3)
            with act.Fori(4, STRIPS) as t:
                iteration(t)
            iteration(STRIPS, (1, 2))
            iteration(STRIPS + 1, (2,))

        @block.vector
        def _(dve):
            links = [0]

            def link(instruction):
                links[0] += 1
                instruction.then_inc(dve_chain, 1)
                dve.wait_ge(dve_chain, links[0])

            dve.memset(ps_s[:, :, :], 0.0)
            dve.memset(xw_a[:, :, :], 0.0)
            dve.memset(xw_b[:, :, :], 0.0)
            dve.wait_ge(weights_in, SETUP_LOADS)
            for kind in range(2):
                for p in range(PH):
                    dve.tensor_tensor(
                        score_bias[:, kind, p, :].rearrange("p (w n) -> p w n", n=N),
                        mask_sb[:, kind, :].rearrange("p (w n) -> p w n", n=N),
                        rpb_sb[:, N * p:N * p + N].unsqueeze(1).to_broadcast([128, NW, N]), ALU.add)
            dve.wait_ge(bias_full, 1)
            for rows, lo, hi, scale in ((128, 0, 4, QKV_SCALE), (64, 4, 5, QKV_SCALE),
                                        (128, 5, 5 + HT, 1.0)):
                link(dve.tensor_tensor(bias[0:rows, lo:hi], ps_w[0:rows, 0, lo:hi],
                                       bias_in[0:rows, lo:hi], ALU.add))
                link(dve.tensor_scalar(bias[0:rows, lo:hi], bias[0:rows, lo:hi], scale, None,
                                       ALU.mult))
            for stage, hi_t, lo_t, part in ((stage_a, wa_hi, wa_lo, 0), (stage_b, wb_hi, wb_lo, 1)):
                for c0, c1, gain, scale in ((OQK, OF1, g1_sb, QKV_SCALE), (OF1, OPJ, g2_sb, W_SCALE),
                                            (OPJ, NWT, None, W_SCALE)):
                    s = stage[:, c0:c1]
                    if gain is None:
                        link(dve.tensor_scalar(s, s, scale, None, ALU.mult))
                    else:
                        link(dve.tensor_scalar(s, s, gain[:, part:part + 1], scale, ALU.mult,
                                               ALU.mult))
                    link(dve.tensor_copy(hi_t[:, c0:c1], s))
                    dve.tensor_tensor(lo_t[:, c0:c1], s, hi_t[:, c0:c1], ALU.subtract)
            link(dve.tensor_scalar(stage_2[:, :], stage_2[:, :], W_SCALE, None, ALU.mult))
            link(dve.tensor_copy(w2_hi[:, :], stage_2[:, :]))
            link(dve.tensor_tensor(w2_lo[:, :], stage_2[:, :], w2_hi[:, :], ALU.subtract))
            for half, part in enumerate((w2_hi, w2_lo)):
                last = dve.tensor_copy(w2_both[:, :, CB * half:CB * half + CB],
                                       part[:, :].rearrange("p (j c) -> p j c", j=HT)[:, :, CA:C])
            last.then_inc(weights_ready, 1)

            def to_windows(t, slot, count):
                dve.wait_ge(x_loaded[slot], count)
                wait(dve, xt_full, 2 * t)
                for src, dst in ((xa[slot], xw_a), (xb[slot], xw_b)):
                    rows = src[:, :].rearrange("p (r c) -> p r c", r=WS)
                    wins = dst[:, :, 0:N].rearrange("p w (r c) -> p w r c", r=WS)
                    dve.tensor_copy(wins[:, 0:NW - 1], rows[:, :, SHIFT:SHIFT + T // WS - WS]
                                    .rearrange("p r (w c) -> p w r c", c=WS))
                    dve.tensor_copy(wins[:, NW - 1, :, 0:WS - SHIFT], rows[:, :, W - WS + SHIFT:W])
                    last = dve.tensor_copy(wins[:, NW - 1, :, WS - SHIFT:WS], rows[:, :, 0:SHIFT])
                last.then_inc(xw_ready, 1)

            def statistics(rows, full, t, banks, stats, mv, chain, done):
                for g in range(4):
                    if g % 2 == 0:
                        dve.wait_ge(full, 2 * t + g // 2 + 1)
                    last = dve.bn_stats(stats[0:rows, g, :],
                                        banks[0:rows, g // 2, (g % 2) * C:(g % 2 + 1) * C])
                last.then_inc(chain, 1)
                dve.wait_ge(chain, t + 1)
                alone(dve, passed_dve)
                for g in range(4):
                    last = dve.bn_aggr(mv[0:rows, g, :], stats[0:rows, g, :])
                last.then_inc(done, 1)

            def probs_lo(u):
                for g in range(NPAIR):
                    dve.wait_ge(pt_hi, 4 * u + g + 1)
                    dve.tensor_tensor(pt_lo_sb[:, g, :, :], bank("pt", g)[:, 0:PH * 128]
                                      .rearrange("p (a n) -> p a n", a=PH), pt_hi_sb[:, g, :, :],
                                      ALU.subtract).then_inc(pt_lo, 1)

            def attended_lo(u):
                dve.wait_ge(o_hi, 2 * u + 2)
                dve.scalar_tensor_tensor(oa_lo[:, :].rearrange("p (b n) -> p b n", b=2),
                                         ps_o[:, :, 0:T // 2], bias[:, 3:4],
                                         oa_hi[:, :].rearrange("p (b n) -> p b n", b=2),
                                         ALU.add, ALU.subtract).then_inc(o_lo, 1)
                dve.scalar_tensor_tensor(o3[CB:128, :].rearrange("p (b n) -> p b n", b=2),
                                         ps_o[0:CB, :, T // 2:T], bias[0:CB, 4:5],
                                         o3[0:CB, :].rearrange("p (b n) -> p b n", b=2),
                                         ALU.add, ALU.subtract).then_inc(o_lo, 1)

            def normed_lo_1(t):
                dve.wait_ge(xn_hi, 2 * t + 1)
                dve.tensor_tensor(xna_lo[:, :, :], bank("nt", 0).rearrange("p (w n) -> p w n", w=NW),
                                  xna_hi[:, :, :], ALU.subtract).then_inc(xn_lo, 1)
                dve.wait_ge(xn_hi, 2 * t + 2)
                dve.tensor_tensor(xn3[CB:128, :, :],
                                  bank("nt", 1)[0:CB, :].rearrange("p (w n) -> p w n", w=NW),
                                  xn3[0:CB, :, :], ALU.subtract).then_inc(xn_lo, 1)

            def queries_keys_lo(t):
                for i, hi, lo in ((0, q_hi, q_lo), (1, k_hi, k_lo)):
                    dve.wait_ge(qk_hi, 3 * t + i + 1)
                    dve.scalar_tensor_tensor(lo[:, :], bank("qk", i)[:, 0:T], bias[:, i:i + 1],
                                             hi[:, :], ALU.add, ALU.subtract).then_inc(qk_lo, 1)
                dve.wait_ge(qk_hi, 3 * t + 3)
                dve.scalar_tensor_tensor(q45_lo[:, :], bank("qk", 2)[0:64, 0:T], bias[0:64, 2:3],
                                         q45_hi[:, :], ALU.add, ALU.subtract)
                dve.scalar_tensor_tensor(k45_lo[:, :], bank("qk", 2)[64:128, 0:T],
                                         bias[64:128, 2:3], k45_hi[:, :], ALU.add,
                                         ALU.subtract).then_inc(qk_lo, 1)

            def values_lo(t, i):
                dve.wait_ge(v_hi_done, 2 * t + i + 1)
                dve.tensor_tensor(v_lo[:, 2 * i:2 * i + 2, :], bank("v", i)[:, 0:2 * C]
                                  .rearrange("p (g c) -> p g c", g=2),
                                  v_hi[:, 2 * i:2 * i + 2, :], ALU.subtract
                                  ).then_inc(v_lo_done, 1)

            def normed_lo_2(u):
                dve.wait_ge(x2_hi, 2 * u + 1)
                dve.tensor_tensor(x2a_lo[:, :], bank("n2", 0)[:, 0:T], x2a_hi[:, :],
                                  ALU.subtract).then_inc(x2_lo, 1)
                dve.wait_ge(x2_hi, 2 * u + 2)
                dve.tensor_tensor(x23[CB:128, :], bank("n2", 1)[0:CB, 0:T], x23[0:CB, :],
                                  ALU.subtract).then_inc(x2_lo, 1)

            def windows(a):
                return a.rearrange("p (w n) -> p w n", n=N)

            def logits_and_max(t, p, kind):
                dve.wait_ge(s_full, PH * t + p + 1)
                wait(dve, p_exp, PH * (t - 1) + p + 1)
                dve.scalar_tensor_tensor(logits[:, p, :], ps_s[:, p, 0:T],
                                         HD ** -0.5 / (QKV_SCALE * QKV_SCALE),
                                         score_bias[:, kind, p, :], ALU.mult, ALU.add
                                         ).then_inc(s_biased, 1)
                dve.wait_ge(s_biased, PH * t + p + 1)
                dve.tensor_reduce(row_max[:, p, :], windows(logits[:, p, :]), AX.X, ALU.max
                                  ).then_inc(s_max, 1)

            def row_sums(t, p):
                dve.wait_ge(p_exp, PH * t + p + 1)
                dve.tensor_reduce(row_sum[:, p, :], windows(expd[:, p, :]), AX.X, ALU.add
                                  ).then_inc(p_sum, 1)
                dve.wait_ge(p_sum, PH * t + p + 1)
                dve.reciprocal(row_inv[:, p, :], row_sum[:, p, :]).then_inc(p_inv, 1)

            def split_hidden(s, items):
                for j in items:
                    dve.wait_ge(gelu_done, HT * s + j + 1)
                    dve.tensor_copy(h_hi[:, j, :], gelu[:, j % 3, :]).then_inc(hh_done, 1)
                    dve.wait_ge(hh_done, HT * s + j + 1)
                    dve.tensor_tensor(h_lo[:, j, :], gelu[:, j % 3, :], h_hi[:, j, :],
                                      ALU.subtract).then_inc(h_ready, 1)

            def contracted(m, slot):
                dve.wait_ge(f2_full, 2 * m + 1)
                wait(dve, out_ready, m)
                dve.scalar_tensor_tensor(f2_a[:, :], bank("f2", 0)[:, 0:T], 1.0 / W_SCALE,
                                         x1_a[slot][:, :], ALU.mult, ALU.add).then_inc(f2_sum, 1)
                dve.wait_ge(f2_full, 2 * m + 2)
                dve.scalar_tensor_tensor(f2_b[:, :], bank("f2", 1)[0:CB, 0:T], 1.0 / W_SCALE,
                                         x1_b[slot][:, :], ALU.mult, ALU.add
                                         ).then_inc(f2_half, 1)
                dve.wait_ge(f2_half, m + 1)
                dve.scalar_tensor_tensor(f2_b[:, :], bank("f2", 1)[CB:128, 0:T], 1.0 / W_SCALE,
                                         f2_b[:, :], ALU.mult, ALU.add).then_inc(f2_sum, 1)

            def iteration(t, slot, kind, stages=(0, 1, 2), count=None):
                front, back, mlp = (n in stages for n in range(3))
                u, m = t - 1, t - 2
                if front:
                    statistics(128, xt_full, t, ps_s, stats1, mv1, stat1_chain, aggr1)
                if back:
                    probs_lo(u)
                if mlp:
                    split_hidden(m, (0, 1, 2, 3, 4))
                if back:
                    attended_lo(u)
                if front:
                    normed_lo_1(t)
                if mlp:
                    split_hidden(m, (5,))
                if front:
                    queries_keys_lo(t)
                    logits_and_max(t, 0, kind)
                    values_lo(t, 0)
                if back:
                    statistics(XG, x1t_full, u, ps_o, stats2, mv2, stat2_chain, aggr2)
                if front:
                    logits_and_max(t, 1, kind)
                    values_lo(t, 1)
                    logits_and_max(t, 2, kind)
                    row_sums(t, 0)
                    row_sums(t, 1)
                if count is not None:
                    to_windows(t + 1, 1 - slot, count)
                if front:
                    row_sums(t, 2)
                if back:
                    normed_lo_2(u)
                if mlp:
                    contracted(m, slot)

            to_windows(0, 0, 64)

            def pairs(t, kind):
                iteration(t, 0, kind, count=32 * t + 64)
                iteration(t + 1, 1, kind, count=32 * t + 128)

            iteration(0, 0, 0, (0,), count=64)
            iteration(1, 1, 0, (0, 1), count=128)
            pairs(2, 0)
            with dve.Fori(4, PLAIN, 2) as t:
                pairs(t, 0)
            with dve.Fori(PLAIN, STRIPS - 2, 2) as t:
                pairs(t, 1)
            iteration(STRIPS - 2, 0, 1, count=32 * STRIPS)
            iteration(STRIPS - 1, 1, 1)
            iteration(STRIPS, 0, 1, (1, 2))
            iteration(STRIPS + 1, 1, 1, (2,))

        @block.gpsimd
        def _(pool):
            pool.memset(eps_sb[:, :], EPS)
            pool.memset(power_sb[:, :], -0.5)
            pool.memset(minus_sb[:, :], -1.0)
            pool.memset(warm[:, :], 0.0)
            pool.memset(probs[:, :, :, :], 0.0).then_inc(consts_ready, 1)
            pool.wait_ge(consts_ready, 1)

            def inverse_deviation(rows, t, aggr, mv, var, rstd, shift, chain, ready):
                pool.wait_ge(aggr, t + 1)
                pool.tensor_tensor(var[0:rows, :], mv[0:rows, :, 1], eps_sb[0:rows, :], ALU.add)
                pool.tensor_tensor(shift[0:rows, :], mv[0:rows, :, 0], minus_sb[0:rows, :],
                                   ALU.mult).then_inc(pool_chain, 1)
                pool.wait_ge(pool_chain, chain + 1)
                pool.tensor_tensor(rstd[0:rows, :], var[0:rows, :], power_sb[0:rows, :],
                                   ALU.pow).then_inc(pool_chain, 1)
                pool.wait_ge(pool_chain, chain + 2)
                pool.tensor_tensor(shift[0:rows, :], shift[0:rows, :], rstd[0:rows, :],
                                   ALU.mult).then_inc(ready, 1)

            def residual(u, slot):
                wait(pool, f2_sum, 2 * (u - 1))
                pool.wait_ge(pj_out, 2 * u + 2)
                for pj, xs, x1 in ((pj_a, xa[slot], x1_a[slot]), (pj_b, xb[slot], x1_b[slot])):
                    pj_r, x_r, x1_r = (a[:, :].rearrange("p (r c) -> p r c", r=WS)
                                       for a in (pj, xs, x1))
                    pool.tensor_tensor(x1_r[:, :, SHIFT:W], pj_r[:, :, 0:CUT], x_r[:, :, SHIFT:W],
                                       ALU.add)
                    last = pool.tensor_tensor(x1_r[:, :, 0:SHIFT], pj_r[:, :, CUT:W],
                                              x_r[:, :, 0:SHIFT], ALU.add)
                last.then_inc(x1_ready, 1)

            def subtract_max(t, p):
                pool.wait_ge(s_max, PH * t + p + 1)
                rows = logits[:, p, :].rearrange("p (w n) -> p w n", n=N)
                pool.tensor_tensor(rows, rows, row_max[:, p, :].unsqueeze(2)
                                   .to_broadcast([128, NW, N]), ALU.subtract
                                   ).then_inc(s_shifted, 1)

            def normalise(t, p):
                pool.wait_ge(p_inv, PH * t + p + 1)
                wait(pool, pt_full, 4 * t)
                pool.tensor_tensor(probs[:, p, :, 0:N],
                                   expd[:, p, :].rearrange("p (w n) -> p w n", n=N),
                                   row_inv[:, p, :].unsqueeze(2).to_broadcast([128, NW, N]),
                                   ALU.mult).then_inc(p_ready, 1)

            def finish(m):
                for i, rows, f2, dst in ((0, CA, f2_a, out_a), (1, CB, f2_b, out_b)):
                    pool.wait_ge(f2_sum, 2 * m + i + 1)
                    if i == 0:
                        wait(pool, out_stored, 64 * m)
                    last = pool.tensor_tensor(dst[:, :], f2[:, :], b_fc2_sb[0:rows, i:i + 1]
                                              .to_broadcast([rows, T]), ALU.add)
                last.then_inc(out_ready, 1)

            def iteration(t, slot, stages=(0, 1, 2), chain=0):
                front, back, mlp = (n in stages for n in range(3))
                u, m = t - 1, t - 2
                if front:
                    inverse_deviation(128, t, aggr1, mv1, var1, rstd1, shift1, chain, rstd1_ready)
                    chain = chain + 2
                if back:
                    residual(u, 1 - slot)
                if front:
                    subtract_max(t, 0)
                if back:
                    inverse_deviation(XG, u, aggr2, mv2, var2, rstd2, shift2, chain, rstd2_ready)
                if front:
                    subtract_max(t, 1)
                    subtract_max(t, 2)
                    for p in range(PH):
                        normalise(t, p)
                if mlp:
                    finish(m)

            iteration(0, 0, (0,))
            iteration(1, 1, (0, 1), chain=2)
            iteration(2, 0, chain=6)
            iteration(3, 1, chain=10)
            with pool.Fori(4, STRIPS, 2) as t:
                iteration(t, 0, chain=4 * t - 2)
                iteration(t + 1, 1, chain=4 * t + 2)
            iteration(STRIPS, 0, (1, 2), chain=4 * STRIPS - 2)
            iteration(STRIPS + 1, 1, (2,))


def kernel(x, L0_conv_qkv_w, L0_conv_qkv_b, L0_conv_proj_w, L0_conv_proj_b, L0_conv_rpb_table,
           L0_conv_norm1_g, L0_conv_norm1_b, L0_conv_norm2_g, L0_conv_norm2_b,
           L0_conv_fc1_w, L0_conv_fc1_b, L0_conv_fc2_w, L0_conv_fc2_b):
    import numpy as np
    import concourse.bacc as bacc
    from concourse.bass_utils import run_bass_kernel_spmd as run

    def lay(a):
        return np.ascontiguousarray(a)

    x = np.asarray(x)
    qkv_w, qkv_b = np.asarray(L0_conv_qkv_w), np.asarray(L0_conv_qkv_b)

    def two_columns(v):
        v = np.asarray(v)
        return lay(np.stack([v[:CA], np.concatenate([v[CA:], v[CA:]])], axis=1))

    order = np.concatenate([np.arange(0, CA), np.arange(C, C + CA),
                            np.arange(CA, C), np.arange(C + CA, 2 * C)])
    r, c = np.divmod(np.arange(N), WS)
    index = (r[:, None] - r[None, :] + WS - 1) * (2 * WS - 1) + (c[:, None] - c[None, :] + WS - 1)
    gathered = np.asarray(L0_conv_rpb_table)[index]
    rpb = np.zeros((128, PH, N), np.float32)
    for h in range(HEADS):
        rpb[NP * (h % 2):NP * (h % 2) + N, h // 2] = gathered[:, :, h]
    late_r, late_c = r >= WS - SHIFT, c >= WS - SHIFT
    mask = np.zeros((128, 2, NW, N), np.float32)
    for kind in range(2):
        for w in range(NW):
            apart = np.zeros((N, N), bool)
            if kind == 1:
                apart |= late_r[:, None] != late_r[None, :]
            if w == NW - 1:
                apart |= late_c[:, None] != late_c[None, :]
            for half in (0, NP):
                mask[half:half + N, kind, w] = np.where(apart, np.float32(-100), np.float32(0))

    fc2_t = np.asarray(L0_conv_fc2_w).T
    arrays = {
        "x": lay(x.reshape(B, C, H * W)),
        "w_qk": lay(qkv_w[order].T),
        "w_v": lay(qkv_w[2 * C:].T),
        "w_proj": lay(np.asarray(L0_conv_proj_w).T),
        "w_fc1": lay(np.asarray(L0_conv_fc1_w).T),
        "w_fc2": lay(fc2_t.reshape(HT, 128, C).transpose(1, 0, 2).reshape(128, HT * C)),
        "b_qk": lay(qkv_b[order].reshape(3, 128).T),
        "b_v": two_columns(qkv_b[2 * C:]),
        "b_proj": two_columns(L0_conv_proj_b),
        "b_fc1": lay(np.asarray(L0_conv_fc1_b).reshape(HT, 128).T),
        "b_fc2": two_columns(L0_conv_fc2_b),
        "g1": two_columns(L0_conv_norm1_g),
        "beta1": two_columns(L0_conv_norm1_b),
        "g2": two_columns(L0_conv_norm2_g),
        "beta2": two_columns(L0_conv_norm2_b),
        "rpb": lay(rpb.reshape(128, PH * N)),
        "mask": lay(mask.reshape(128, 2, T)),
        "ident": np.eye(128, dtype=np.float32),
    }
    nc = bacc.Bacc("TRN2", target_bir_lowering=False, num_devices=1)
    args = [nc.dram_tensor(f"in_{k}", a.shape, mybir.dt.from_np(a.dtype), kind="ExternalInput").ap()
            for k, a in arrays.items()]
    result = nc.dram_tensor("out_dram", (B, C, H * W), mybir.dt.float32, kind="ExternalOutput").ap()
    swin_block(nc, *args, result)
    r = run(nc, [{f"in_{k}": a for k, a in arrays.items()}], core_ids=[0])
    return r.results[0]["out_dram"].reshape(B, C, H, W)
```

```python
import concourse.bass as bass
from concourse import mybir
from contextlib import ExitStack

B, C, H, W = 16, 192, 56, 56
WS, SHIFT, HEADS, HID = 7, 3, 6, 768
EPS = 1e-5
HD = C // HEADS
N = WS * WS
NP = 64
NW = W // WS
NPAIR = NW // 2
T = WS * W
ROWS = H // WS
STRIPS = B * ROWS
PLAIN = B * (ROWS - 1)
CA, CB = 128, 64
PH = HEADS // 2
XG = T // 4
HT = HID // 128
QKV_SCALE, W_SCALE = 16.0, 64.0
SETUP_LOADS = 16 * 25
WIDE = 512
CUT = W - SHIFT


def swin_block(nc, x, w_qk, w_v, w_proj, w_fc1, w_fc2, b_qk, b_v, b_proj, b_fc1, b_fc2,
               g1, beta1, g2, beta2, rpb, mask, ident, out):
    f32, f16 = mybir.dt.float32, mybir.dt.float16
    ALU, ACT, AX = mybir.AluOpType, mybir.ActivationFunctionType, mybir.AxisListType
    ctx = ExitStack()
    with ctx:
        def sb(name, shape, dt=f32):
            return ctx.enter_context(nc.sbuf_tensor(name, shape, dt))

        def sem(name):
            return ctx.enter_context(nc.semaphore(name))

        ident_sb = sb("ident_sb", [128, 128])
        eps_sb = sb("eps_sb", [128, 4])
        power_sb = sb("power_sb", [128, 4])
        minus_sb = sb("minus_sb", [128, 4])
        g1_sb, beta1_sb = sb("g1_sb", [128, 2]), sb("beta1_sb", [128, 2])
        g2_sb, beta2_sb = sb("g2_sb", [128, 2]), sb("beta2_sb", [128, 2])
        stage_a = sb("stage_a", [128, 3 * C + HID + C])
        stage_b = sb("stage_b", [128, 3 * C + HID + C])
        stage_2 = sb("stage_2", [128, HT * C])
        NWT = 3 * C + HID + C
        OQK, OV, OF1, OPJ = 0, 2 * C, 3 * C, 3 * C + HID
        wa_hi, wa_lo = sb("wa_hi", [128, NWT], f16), sb("wa_lo", [128, NWT], f16)
        wb_hi, wb_lo = sb("wb_hi", [128, NWT], f16), sb("wb_lo", [128, NWT], f16)
        w2_hi, w2_lo = sb("w2_hi", [128, HT * C], f16), sb("w2_lo", [128, HT * C], f16)
        w2_both = sb("w2_both", [128, HT, 128], f16)
        bias_in = sb("bias_in", [128, 5 + HT])
        bias = sb("bias", [128, 5 + HT])
        b_proj_sb = sb("b_proj_sb", [128, 2])
        b_fc2_sb = sb("b_fc2_sb", [128, 2])
        rpb_sb = sb("rpb_sb", [128, PH * N])
        mask_sb = sb("mask_sb", [128, 2, T])
        score_bias = sb("score_bias", [128, 2, PH, T])

        xa = [sb(f"xa{i}", [CA, T]) for i in range(2)]
        xb = [sb(f"xb{i}", [CB, T]) for i in range(2)]
        xw_a, xw_b = sb("xw_a", [CA, NW, NP]), sb("xw_b", [CB, NW, NP])
        stats1, mv1 = sb("stats1", [128, NPAIR, 6]), sb("mv1", [128, NPAIR, 2])
        var1, rstd1, shift1 = sb("var1", [128, 4]), sb("rstd1", [128, 4]), sb("shift1", [128, 4])
        xn_tok = sb("xn_tok", [128, NPAIR, C])
        xna_hi, xna_lo = sb("xna_hi", [CA, NW, NP], f16), sb("xna_lo", [CA, NW, NP], f16)
        xn3 = sb("xn3", [128, NW, NP], f16)
        q_hi, q_lo = sb("q_hi", [128, T], f16), sb("q_lo", [128, T], f16)
        k_hi, k_lo = sb("k_hi", [128, T], f16), sb("k_lo", [128, T], f16)
        q45_hi, q45_lo = sb("q45_hi", [64, T], f16), sb("q45_lo", [64, T], f16)
        k45_hi, k45_lo = sb("k45_hi", [64, T], f16), sb("k45_lo", [64, T], f16)
        v_hi, v_lo = sb("v_hi_sb", [128, NPAIR, C], f16), sb("v_lo_sb", [128, NPAIR, C], f16)
        logits = sb("logits", [128, PH, T])
        expd = sb("expd", [128, PH, T])
        row_max, row_sum = sb("row_max", [128, PH, NW]), sb("row_sum", [128, PH, NW])
        row_inv = sb("row_inv", [128, PH, NW])
        probs = sb("probs", [128, PH, NW, NP])
        pt_hi_sb = sb("pt_hi_sb", [128, NPAIR, PH * 2, N], f16)
        pt_lo_sb = sb("pt_lo_sb", [128, NPAIR, PH * 2, N], f16)
        oa_hi, oa_lo = sb("oa_hi", [128, T], f16), sb("oa_lo", [128, T], f16)
        o3 = sb("o3", [128, T], f16)
        pj_a, pj_b = sb("pj_a", [CA, T]), sb("pj_b", [CB, T])
        x1_a = [sb(f"x1_a{i}", [CA, T]) for i in range(2)]
        x1_b = [sb(f"x1_b{i}", [CB, T]) for i in range(2)]
        stats2, mv2 = sb("stats2", [128, 4, 6]), sb("mv2", [128, 4, 2])
        var2, rstd2, shift2 = sb("var2", [128, 4]), sb("rstd2", [128, 4]), sb("shift2", [128, 4])
        x2_tok = sb("x2_tok", [XG, 4, C])
        x2a_hi, x2a_lo = sb("x2a_hi", [CA, T], f16), sb("x2a_lo", [CA, T], f16)
        x23 = sb("x23", [128, T], f16)
        warm = sb("warm", [1, 3])
        gelu = sb("gelu", [128, 3, T])
        h_hi, h_lo = sb("h_hi", [128, HT, T], f16), sb("h_lo", [128, HT, T], f16)
        f2_a, f2_b = sb("f2_a", [CA, T]), sb("f2_b", [CB, T])
        out_a, out_b = sb("out_a", [CA, T]), sb("out_b", [CB, T])

        ps_s = ctx.enter_context(nc.psum_tensor("ps_s", [128, PH, WIDE], f32))
        ps_o = ctx.enter_context(nc.psum_tensor("ps_o", [128, 2, WIDE], f32))
        ps_w = ctx.enter_context(nc.psum_tensor("ps_w", [128, 3, WIDE], f32))

        weights_in = sem("weights_in")
        bias_full = sem("bias_full")
        weights_ready = sem("weights_ready")
        dve_chain = sem("dve_chain")
        consts_ready = sem("consts_ready")
        x_loaded = [sem("x_loaded0"), sem("x_loaded1")]
        xw_ready = sem("xw_ready")
        xt_full = sem("xt_full")
        aggr1 = sem("aggr1")
        stat1_chain = sem("stat1_chain")
        pool_chain = sem("pool_chain")
        rstd1_ready = sem("rstd1_ready")
        norm1 = sem("norm1")
        nt_full = sem("nt_full")
        xn_hi, xn_lo = sem("xn_hi"), sem("xn_lo")
        qk_full = sem("qk_full")
        qk_hi, qk_lo = sem("qk_hi"), sem("qk_lo")
        v_full = sem("v_full")
        v_hi_done, v_lo_done = sem("v_hi_done"), sem("v_lo_done")
        s_full = sem("s_full")
        s_biased = sem("s_biased")
        s_max = sem("s_max")
        s_shifted = sem("s_shifted")
        p_exp = sem("p_exp")
        p_sum = sem("p_sum")
        p_inv = sem("p_inv")
        p_ready = sem("p_ready")
        pt_full = sem("pt_full")
        pt_hi, pt_lo = sem("pt_hi"), sem("pt_lo")
        o_full = sem("o_full")
        o_hi, o_lo = sem("o_hi"), sem("o_lo")
        pj_full = sem("pj_full")
        pj_out = sem("pj_out")
        x1_ready = sem("x1_ready")
        x1t_full = sem("x1t_full")
        stat2_chain = sem("stat2_chain")
        aggr2 = sem("aggr2")
        rstd2_ready = sem("rstd2_ready")
        norm2 = sem("norm2")
        n2_full = sem("n2_full")
        x2_hi, x2_lo = sem("x2_hi"), sem("x2_lo")
        f1_full = sem("f1_full")
        gelu_done = sem("gelu_done")
        hh_done = sem("hh_done")
        h_ready = sem("h_ready")
        f2_full = sem("f2_full")
        f2_half = sem("f2_half")
        f2_sum = sem("f2_sum")
        out_ready = sem("out_ready")
        out_stored = sem("out_stored")

        passed_pe, passed_dve = sem("passed_pe"), sem("passed_dve")

        def wait(eng, semaphore, value):
            if not isinstance(value, int) or value > 0:
                eng.wait_ge(semaphore, value)

        def alone(eng, marks):
            eng.sem_inc(marks, 1)

        KINDS = [("pt", 0, 2, 1, (pt_hi, pt_lo), NPAIR),
                 ("f1", 3, 1, 2, (gelu_done,), HT),
                 ("pt", 2, 2, 1, (pt_hi, pt_lo), NPAIR),
                 ("f1", 4, 2, 2, (gelu_done,), HT),
                 ("nt", 0, 2, 0, (xn_hi, xn_lo), 2),
                 ("pj", 0, 2, 1, (pj_out,), 2),
                 ("qk", 0, 3, 0, (qk_hi, qk_lo), 3),
                 ("v", 0, 1, 0, (v_hi_done, v_lo_done), 2),
                 ("f2", 0, 2, 2, (f2_sum,), 2),
                 ("v", 1, 1, 0, (v_hi_done, v_lo_done), 2)]
        JOBS = [(k, first + i, lag, done, per) for k, first, n, lag, done, per in KINDS
                for i in range(n)]
        PLACE = {(k, i): p for p, (k, i, *_) in enumerate(JOBS)}
        assert len(JOBS) % 3 == 0

        def bank(kind, i):
            if kind == "f1" and i < 3:
                return ps_s[:, i, :]
            if kind == "n2":
                return ps_o[:, i, :]
            return ps_w[:, PLACE[kind, i] % 3, :]

        def queries(a):
            return a[:, 0:HEADS * NP].rearrange("p (h n) -> p h n", h=HEADS)[:, :, 0:N]

        def tokens(a):
            return a.rearrange("p (w n) -> p w n", w=NW)[:, :, 0:N]

        def wait_bank(eng, kind, i, t, stages):
            mine = PLACE[kind, i]
            before = [(p, 0) for p in range(mine - 3, -1, -3)]
            before += [(p, 1) for p in range(len(JOBS) - 1, -1, -1) if p % 3 == mine % 3]
            for p, ago in before:
                _, j, lag, done, per = JOBS[p]
                if ago == 0 and lag not in stages:
                    continue
                if isinstance(t, int) and t - ago - lag >= STRIPS:
                    continue
                for semaphore in done:
                    wait(eng, semaphore, (t - ago - lag) * per + j + 1)
                return

        block = ctx.enter_context(nc.Block())

        def dram_rows(tensor, b, c0, c1, row, rows):
            return tensor[bass.ds(b, 1), c0:c1, row * W:(row + rows) * W].rearrange("b c n -> (b c) n")

        def strip_parts(i):
            return [(WS * i + SHIFT, 4, 0), ((WS * i + SHIFT + 4) % H, 3, 4 * W)]

        @block.sync
        def _(sp):
            def load(b, i, slot):
                for row, rows, at in strip_parts(i):
                    sp.dma_start(xa[slot][:, at:at + rows * W],
                                 dram_rows(x, b, 0, CA, row, rows)).then_inc(x_loaded[slot], 16)
                    sp.dma_start(xb[slot][:, at:at + rows * W],
                                 dram_rows(x, b, CA, C, row, rows)).then_inc(x_loaded[slot], 16)

            def store(b, i):
                for row, rows, at in strip_parts(i):
                    sp.dma_start(dram_rows(out, b, 0, CA, row, rows),
                                 out_a[:, at:at + rows * W]).then_inc(out_stored, 16)
                    sp.dma_start(dram_rows(out, b, CA, C, row, rows),
                                 out_b[:, at:at + rows * W]).then_inc(out_stored, 16)

            def step(s, this, later, slot):
                if later is not None:
                    sp.wait_ge(x1_ready, s + 2)
                    load(*later, slot)
                sp.wait_ge(out_ready, s + 1)
                store(*this)

            load(0, 0, 0)
            load(0, 1, 1)
            sp.wait_ge(x1_ready, 1)
            load(0, 2, 0)
            per = ROWS - 1
            two = 2 * per

            def two_images(b, s):
                for k in range(two):
                    if k + 3 < two:
                        later = (b + (k + 3) // per, (k + 3) % per)
                    elif isinstance(b, int) and b + 2 >= B:
                        later = (k + 3 - two, ROWS - 1)
                    else:
                        later = (b + 2, k + 3 - two)
                    step(s + k, (b + k // per, k % per), later, (k + 1) % 2)

            with sp.Fori(0, B // 2 - 1) as b2:
                two_images(b2 * 2, b2 * two)
            two_images(B - 2, PLAIN - two)
            with sp.Fori(0, B // 2 - 2) as b2:
                for k in range(2):
                    step(b2 * 2 + (PLAIN + k), (b2 * 2 + k, ROWS - 1),
                         (b2 * 2 + (k + 3), ROWS - 1), (k + 1) % 2)
            for b in range(B - 4, B):
                later = (b + 3, ROWS - 1) if b + 3 < B else None
                step(PLAIN + b, (b, ROWS - 1), later, (b + 1) % 2)
            sp.wait_ge(out_stored, 64 * STRIPS)

        @block.tensor
        def _(pe):
            def five(dst, lhs_rhs):
                for n, (lhs, rhs) in enumerate(lhs_rhs):
                    last = nc.tensor.matmul(dst, lhs, rhs, start=n == 0, stop=n == 4)
                return last

            def weights_moving(dst, a_hi, a_lo, three, col, n):
                cols = slice(col, col + n)
                return five(dst, [(a_hi, wa_hi[:, cols]), (a_hi, wa_lo[:, cols]),
                                  (a_lo, wa_hi[:, cols]), (three, wb_hi[:, cols]),
                                  (three, wb_lo[:, cols])])

            def weights_still(dst, a_hi, a_lo, three, col, n):
                cols = slice(col, col + n)
                return five(dst, [(wa_hi[:, cols], a_hi), (wa_hi[:, cols], a_lo),
                                  (wa_lo[:, cols], a_hi), (wb_hi[:, cols], three),
                                  (wb_lo[:, cols], three)])

            pe.wait_ge(weights_in, SETUP_LOADS)
            cols = [(OQK, 128, beta1_sb), (OQK + 128, 128, beta1_sb), (OQK + 256, 128, beta1_sb),
                    (OV, 128, beta1_sb), (OV + 128, 64, beta1_sb)]
            cols += [(OF1 + 128 * j, 128, beta2_sb) for j in range(HT)]
            for n, (col, m, beta) in enumerate(cols):
                nc.tensor.matmul(ps_w[0:m, 0, n:n + 1], stage_a[:, col:col + m], beta[:, 0:1],
                                 start=True, stop=False)
                last = nc.tensor.matmul(ps_w[0:m, 0, n:n + 1], stage_b[0:CB, col:col + m],
                                        beta[0:CB, 1:2], start=False, stop=True)
            last.then_inc(bias_full, 1)
            pe.wait_ge(weights_ready, 1)

            def to_tokens_1(t, i):
                pe.wait_ge(xw_ready, t + 1)
                wait(pe, gelu_done, HT * (t - 2) + i + 1)
                for g in (2 * i, 2 * i + 1):
                    dst = ps_s[:, i, (g % 2) * C:(g % 2 + 1) * C]
                    nc.tensor.transpose(dst[:, 0:CA], xw_a[:, 2 * g:2 * g + 2, :], ident_sb[:, :])
                    last = nc.tensor.transpose(dst[:, CA:C], xw_b[:, 2 * g:2 * g + 2, :],
                                               ident_sb[0:CB, 0:CB])
                last.then_inc(xt_full, 1)

            def to_channels_1(t, i, stages):
                pe.wait_ge(norm1, 4 * t + 4)
                wait_bank(pe, "nt", i, t, stages)
                alone(pe, passed_pe)
                c0, m = ((0, CA), (CA, CB))[i]
                for g in range(NPAIR):
                    last = nc.tensor.transpose(bank("nt", i)[0:m, 128 * g:128 * g + 128],
                                               xn_tok[:, g, c0:c0 + m], ident_sb[:, :])
                last.then_inc(nt_full, 1)

            def queries_keys(t, i, stages):
                pe.wait_ge(xn_hi, 2 * t + 2)
                pe.wait_ge(xn_lo, 2 * t + 2)
                wait_bank(pe, "qk", i, t, stages)
                dst = bank("qk", i)[:, 0:T].rearrange("p (w n) -> p w n", n=N)
                weights_still(dst, xna_hi[:, :, 0:N], xna_lo[:, :, 0:N], xn3[:, :, 0:N],
                              OQK + 128 * i, 128).then_inc(qk_full, 1)

            def values(t, i, stages):
                pe.wait_ge(xn_hi, 2 * t + 2)
                pe.wait_ge(xn_lo, 2 * t + 2)
                wait_bank(pe, "v", i, t, stages)
                for g in (2 * i, 2 * i + 1):
                    pair = slice(2 * g, 2 * g + 2)
                    last = weights_moving(bank("v", i)[:, (g % 2) * C:(g % 2 + 1) * C],
                                          xna_hi[:, pair, :], xna_lo[:, pair, :],
                                          xn3[:, pair, :], OV, C)
                last.then_inc(v_full, 1)

            def scores(t, p):
                done = 3 if p == PH - 1 else 2
                pe.wait_ge(qk_hi, 3 * t + done)
                pe.wait_ge(qk_lo, 3 * t + done)
                if p == PH - 1:
                    wait(pe, gelu_done, HT * (t - 2) + 3)
                qh, ql, kh, kl = (q_hi, q_lo, k_hi, k_lo) if p < 2 else \
                    (q45_hi, q45_lo, k45_hi, k45_lo)
                for w in range(NW):
                    win = slice(w * N, w * N + N)
                    for n in range(3):
                        for par in range(2):
                            r = HD * ((2 * p + par) % 4)
                            lhs, rhs = ((qh, kh), (qh, kl), (ql, kh))[n]
                            last = nc.tensor.matmul(ps_s[NP * par:NP * par + N, p, win],
                                                    lhs[r:r + HD, win], rhs[r:r + HD, win],
                                                    start=n == 0, stop=n == 2,
                                                    skip_group_check=True)
                last.then_inc(s_full, 1)

            def turn_probs(u, g, stages):
                pe.wait_ge(p_ready, PH * u + PH)
                wait_bank(pe, "pt", g, u + 1, stages)
                for p in range(PH):
                    last = nc.tensor.transpose(bank("pt", g)[:, 128 * p:128 * p + 128],
                                               probs[:, p, 2 * g:2 * g + 2, :], ident_sb[:, :])
                last.then_inc(pt_full, 1)

            def attend(u, g):
                pe.wait_ge(v_hi_done, 2 * u + 2)
                pe.wait_ge(v_lo_done, 2 * u + 2)
                pe.wait_ge(pt_hi, 4 * u + g + 1)
                pe.wait_ge(pt_lo, 4 * u + g + 1)
                alone(pe, passed_pe)
                for heads in (range(4), range(4, HEADS)):
                    for n in range(3):
                        vs, ps = ((v_hi, pt_hi_sb), (v_hi, pt_lo_sb), (v_lo, pt_hi_sb))[n]
                        for odd in range(2):
                            rows = slice(NP * odd, NP * odd + N)
                            for h in heads:
                                col = (T // 2) * (h // 4) + g * N
                                last = nc.tensor.matmul(
                                    ps_o[HD * (h % 4):HD * (h % 4) + HD, odd, col:col + N],
                                    vs[rows, g, HD * h:HD * h + HD],
                                    ps[rows, g, h, :],
                                    start=n == 0, stop=n == 2, skip_group_check=True)
                if g == NPAIR - 1:
                    last.then_inc(o_full, 1)

            def project(u, i, stages):
                pe.wait_ge(o_hi, 2 * u + 2)
                pe.wait_ge(o_lo, 2 * u + 2)
                m = (CA, CB)[i]
                wait_bank(pe, "pj", i, u + 1, stages)
                weights_still(bank("pj", i)[0:m, 0:T], oa_hi[:, :], oa_lo[:, :], o3[:, :],
                              OPJ + CA * i, m).then_inc(pj_full, 1)

            def to_tokens_2(u, i, slot):
                pe.wait_ge(x1_ready, u + 1)
                for g in (2 * i, 2 * i + 1):
                    dst = ps_o[0:XG, i, (g % 2) * C:(g % 2 + 1) * C]
                    cols = slice(XG * g, XG * g + XG)
                    nc.tensor.transpose(dst[:, 0:CA], x1_a[slot][:, cols], ident_sb[:, :])
                    last = nc.tensor.transpose(dst[:, CA:C], x1_b[slot][:, cols],
                                               ident_sb[0:CB, 0:CB])
                last.then_inc(x1t_full, 1)

            def to_channels_2(u, i):
                pe.wait_ge(norm2, 4 * u + 4)
                alone(pe, passed_pe)
                c0, m = ((0, CA), (CA, CB))[i]
                for g in range(4):
                    last = nc.tensor.transpose(bank("n2", i)[0:m, XG * g:XG * g + XG],
                                               x2_tok[:, g, c0:c0 + m], ident_sb[0:XG, 0:XG])
                last.then_inc(n2_full, 1)

            def hidden_item(j):
                weights_still(bank("f1", j)[:, 0:T], x2a_hi[:, :], x2a_lo[:, :], x23[:, :],
                              OF1 + 128 * j, 128).then_inc(f1_full, 1)

            def hidden_first(u, j, stages):
                pe.wait_ge(x2_hi, 2 * u + 2)
                pe.wait_ge(x2_lo, 2 * u + 2)
                if 0 in stages:
                    pe.wait_ge(s_biased, PH * (u + 1) + j + 1)
                hidden_item(j)

            def hidden_rest(m, j, stages):
                wait_bank(pe, "f1", j, m + 2, stages)
                hidden_item(j)

            def contract(m, j, stages):
                if j == 0:
                    for i in range(2):
                        wait_bank(pe, "f2", i, m + 2, stages)
                pe.wait_ge(h_ready, HT * m + j + 1)
                cols = slice(C * j, C * j + CA)
                for n, (w2, hh) in enumerate(((w2_hi, h_hi), (w2_hi, h_lo), (w2_lo, h_hi))):
                    last = nc.tensor.matmul(bank("f2", 0)[:, 0:T], w2[:, cols], hh[:, j, :],
                                            start=j == 0 and n == 0, stop=j == HT - 1 and n == 2)
                if j == HT - 1:
                    last.then_inc(f2_full, 1)
                for n, hh in enumerate((h_hi, h_lo)):
                    last = nc.tensor.matmul(bank("f2", 1)[:, 0:T], w2_both[:, j, :], hh[:, j, :],
                                            start=j == 0 and n == 0, stop=j == HT - 1 and n == 1)
                if j == HT - 1:
                    last.then_inc(f2_full, 1)

            def iteration(t, slot, stages=(0, 1, 2)):
                front, back, mlp = (n in stages for n in range(3))
                u, m = t - 1, t - 2
                if front:
                    to_tokens_1(t, 0)
                if back:
                    turn_probs(u, 0, stages)
                if front:
                    to_tokens_1(t, 1)
                if back:
                    turn_probs(u, 1, stages)
                if mlp:
                    hidden_rest(m, 3, stages)
                if back:
                    attend(u, 0)
                    for i in (2, 3):
                        turn_probs(u, i, stages)
                    attend(u, 1)
                if mlp:
                    hidden_rest(m, 4, stages)
                if back:
                    for i in (2, 3):
                        attend(u, i)
                if mlp:
                    hidden_rest(m, 5, stages)
                if front:
                    for i in (0, 1):
                        to_channels_1(t, i, stages)
                if back:
                    for i in (0, 1):
                        project(u, i, stages)
                if front:
                    for i in (0, 1, 2):
                        queries_keys(t, i, stages)
                    values(t, 0, stages)
                    scores(t, 0)
                if back:
                    for i in (0, 1):
                        to_tokens_2(u, i, 1 - slot)
                if front:
                    scores(t, 1)
                if mlp:
                    contract(m, 0, stages)
                if front:
                    scores(t, 2)
                if mlp:
                    for i in (1, 2, 3):
                        contract(m, i, stages)
                if front:
                    values(t, 1, stages)
                if back:
                    for i in (0, 1):
                        to_channels_2(u, i)
                if mlp:
                    for i in (4, 5):
                        contract(m, i, stages)
                if back:
                    for i in (0, 1, 2):
                        hidden_first(u, i, stages)

            iteration(0, 0, (0,))
            iteration(1, 1, (0, 1))
            iteration(2, 0)
            iteration(3, 1)
            with pe.Fori(4, STRIPS, 2) as t:
                iteration(t, 0)
                iteration(t + 1, 1)
            iteration(STRIPS, 0, (1, 2))
            iteration(STRIPS + 1, 1, (2,))

        @block.scalar
        def _(act):
            ID = ACT.Identity

            act.dma_start(stage_a[:, OQK:OV], w_qk[0:CA, :]).then_inc(weights_in, 16)
            act.dma_start(stage_a[:, OV:OF1], w_v[0:CA, :]).then_inc(weights_in, 16)
            act.dma_start(stage_a[:, OF1:OPJ], w_fc1[0:CA, :]).then_inc(weights_in, 16)
            act.dma_start(stage_a[:, OPJ:NWT], w_proj[0:CA, :]).then_inc(weights_in, 16)
            for half in range(2):
                rows = slice(CB * half, CB * half + CB)
                act.dma_start(stage_b[rows, OQK:OV], w_qk[CA:C, :]).then_inc(weights_in, 16)
                act.dma_start(stage_b[rows, OV:OF1], w_v[CA:C, :]).then_inc(weights_in, 16)
                act.dma_start(stage_b[rows, OF1:OPJ], w_fc1[CA:C, :]).then_inc(weights_in, 16)
                act.dma_start(stage_b[rows, OPJ:NWT], w_proj[CA:C, :]).then_inc(weights_in, 16)
            act.dma_start(stage_2[:, :], w_fc2).then_inc(weights_in, 16)
            for dst, src in ((g1_sb, g1), (beta1_sb, beta1), (g2_sb, g2), (beta2_sb, beta2),
                             (b_proj_sb, b_proj), (b_fc2_sb, b_fc2), (rpb_sb, rpb),
                             (ident_sb, ident)):
                act.dma_start(dst[:, :], src).then_inc(weights_in, 16)
            act.dma_start(mask_sb[:, :, :], mask).then_inc(weights_in, 16)
            act.dma_start(bias_in[:, 0:3], b_qk).then_inc(weights_in, 16)
            act.dma_start(bias_in[:, 3:5], b_v).then_inc(weights_in, 16)
            act.dma_start(bias_in[:, 5:5 + HT], b_fc1).then_inc(weights_in, 16)
            act.wait_ge(weights_ready, 1)
            act.wait_ge(consts_ready, 1)

            def normalise_1(t, groups):
                act.wait_ge(rstd1_ready, t + 1)
                for g in groups:
                    act.activation(xn_tok[:, g, :], ps_s[:, g // 2, (g % 2) * C:(g % 2 + 1) * C], ID,
                                   bias=shift1[:, g:g + 1], scale=rstd1[:, g:g + 1]).then_inc(norm1, 1)

            def probs_hi(u, pairs):
                for g in pairs:
                    act.wait_ge(pt_full, 4 * u + g + 1)
                    act.copy(pt_hi_sb[:, g, :, :], queries(bank("pt", g))).then_inc(pt_hi, 1)

            def attended_hi(u):
                act.wait_ge(o_full, u + 1)
                act.activation(oa_hi[:, :].rearrange("p (b n) -> p b n", b=2), ps_o[:, :, 0:T // 2], ID,
                               bias=bias[:, 3:4]).then_inc(o_hi, 1)
                act.activation(o3[0:CB, :].rearrange("p (b n) -> p b n", b=2),
                               ps_o[0:CB, :, T // 2:T], ID, bias=bias[0:CB, 4:5]).then_inc(o_hi, 1)

            def normed_hi_1(t, halves):
                for i in halves:
                    m, dst = ((CA, xna_hi), (CB, xn3))[i]
                    act.wait_ge(nt_full, 2 * t + i + 1)
                    act.copy(dst[0:m, :, 0:N], tokens(bank("nt", i)[0:m, :])).then_inc(xn_hi, 1)

            def projected(u, halves):
                for i in halves:
                    m, dst = ((CA, pj_a), (CB, pj_b))[i]
                    act.wait_ge(pj_full, 2 * u + i + 1)
                    wait(act, x1_ready, u)
                    rolled = dst[:, :].rearrange("p (r w b c) -> p b w r c", r=WS, b=2, c=WS)
                    src = bank("pj", i)[0:m, 0:T].rearrange("p (b w r c) -> p b w r c", b=2,
                                                            r=WS, c=WS)
                    for odd in range(2):
                        last = act.activation(rolled[:, odd], src[:, odd], ID,
                                              bias=b_proj_sb[0:m, i:i + 1],
                                              scale=1.0 / (QKV_SCALE * W_SCALE))
                    last.then_inc(pj_out, 1)

            def queries_keys_hi(t, tiles):
                for i in tiles:
                    act.wait_ge(qk_full, 3 * t + i + 1)
                    if i < 2:
                        act.activation((q_hi, k_hi)[i][:, :], bank("qk", i)[:, 0:T], ID,
                                       bias=bias[:, i:i + 1]).then_inc(qk_hi, 1)
                    else:
                        act.activation(q45_hi[:, :], bank("qk", 2)[0:64, 0:T], ID,
                                       bias=bias[0:64, 2:3])
                        act.activation(k45_hi[:, :], bank("qk", 2)[64:128, 0:T], ID,
                                       bias=bias[64:128, 2:3]).then_inc(qk_hi, 1)

            def values_hi(t, i):
                act.wait_ge(v_full, 2 * t + i + 1)
                act.copy(v_hi[:, 2 * i:2 * i + 2, :], bank("v", i)[:, 0:2 * C]
                         .rearrange("p (g c) -> p g c", g=2)).then_inc(v_hi_done, 1)

            def normalise_2(u):
                act.wait_ge(rstd2_ready, u + 1)
                for g in range(4):
                    act.activation(x2_tok[:, g, :], ps_o[0:XG, g // 2, (g % 2) * C:(g % 2 + 1) * C],
                                   ID, bias=shift2[0:XG, g:g + 1],
                                   scale=rstd2[0:XG, g:g + 1]).then_inc(norm2, 1)

            def normed_hi_2(u, halves):
                for i in halves:
                    m, dst = ((CA, x2a_hi), (CB, x23))[i]
                    act.wait_ge(n2_full, 2 * u + i + 1)
                    act.copy(dst[0:m, :], bank("n2", i)[0:m, 0:T]).then_inc(x2_hi, 1)

            def activate(s, items):
                for j in items:
                    act.wait_ge(f1_full, HT * s + j + 1)
                    wait(act, h_ready, HT * s + j - 2)
                    act.activation(gelu[:, j % 3, :], bank("f1", j)[:, 0:T], ACT.Gelu,
                                   bias=bias[:, 5 + j:6 + j], scale=1.0 / W_SCALE
                                   ).then_inc(gelu_done, 1)

            def exponent(t, p):
                act.wait_ge(s_shifted, PH * t + p + 1)
                wait(act, p_ready, PH * (t - 1) + p + 1)
                act.activation(expd[:, p, :], logits[:, p, :], ACT.Exp).then_inc(p_exp, 1)

            def load_table(function, at):
                act.activation(warm[:, at:at + 1], warm[:, 0:1], function)

            def iteration(t, stages=(0, 1, 2)):
                front, back, mlp = (n in stages for n in range(3))
                u, m = t - 1, t - 2
                if back:
                    probs_hi(u, (0, 1))
                if mlp:
                    activate(m, (3,))
                if back:
                    probs_hi(u, (2, 3))
                if front:
                    normalise_1(t, (0, 1, 2, 3))
                if back:
                    attended_hi(u)
                if mlp:
                    activate(m, (4, 5))
                if front:
                    normed_hi_1(t, (0, 1))
                if back:
                    projected(u, (0, 1))
                if front:
                    queries_keys_hi(t, (0, 1, 2))
                    values_hi(t, 0)
                    load_table(ACT.Exp, 2)
                if back:
                    normalise_2(u)
                if front:
                    for i in (0, 1):
                        exponent(t, i)
                if back:
                    normed_hi_2(u, (0, 1))
                if front:
                    exponent(t, 2)
                    values_hi(t, 1)
                if back:
                    load_table(ACT.Gelu, 1)
                    activate(u, (0, 1, 2))

            iteration(0, (0,))
            iteration(1, (0, 1))
            iteration(2)
            iteration(3)
            with act.Fori(4, STRIPS) as t:
                iteration(t)
            iteration(STRIPS, (1, 2))
            iteration(STRIPS + 1, (2,))

        @block.vector
        def _(dve):
            links = [0]

            def link(instruction):
                links[0] += 1
                instruction.then_inc(dve_chain, 1)
                dve.wait_ge(dve_chain, links[0])

            dve.memset(ps_s[:, :, :], 0.0)
            dve.memset(xw_a[:, :, :], 0.0)
            dve.memset(xw_b[:, :, :], 0.0)
            for pads in (xna_hi, xna_lo, xn3):
                dve.memset(pads[:, :, N:NP], 0.0)
            dve.wait_ge(weights_in, SETUP_LOADS)
            for kind in range(2):
                for p in range(PH):
                    dve.tensor_tensor(
                        score_bias[:, kind, p, :].rearrange("p (w n) -> p w n", n=N),
                        mask_sb[:, kind, :].rearrange("p (w n) -> p w n", n=N),
                        rpb_sb[:, N * p:N * p + N].unsqueeze(1).to_broadcast([128, NW, N]), ALU.add)
            dve.wait_ge(bias_full, 1)
            for rows, lo, hi, scale in ((128, 0, 4, QKV_SCALE), (64, 4, 5, QKV_SCALE),
                                        (128, 5, 5 + HT, 1.0)):
                link(dve.tensor_tensor(bias[0:rows, lo:hi], ps_w[0:rows, 0, lo:hi],
                                       bias_in[0:rows, lo:hi], ALU.add))
                link(dve.tensor_scalar(bias[0:rows, lo:hi], bias[0:rows, lo:hi], scale, None,
                                       ALU.mult))
            for stage, hi_t, lo_t, part in ((stage_a, wa_hi, wa_lo, 0), (stage_b, wb_hi, wb_lo, 1)):
                for c0, c1, gain, scale in ((OQK, OF1, g1_sb, QKV_SCALE), (OF1, OPJ, g2_sb, W_SCALE),
                                            (OPJ, NWT, None, W_SCALE)):
                    s = stage[:, c0:c1]
                    if gain is None:
                        link(dve.tensor_scalar(s, s, scale, None, ALU.mult))
                    else:
                        link(dve.tensor_scalar(s, s, gain[:, part:part + 1], scale, ALU.mult,
                                               ALU.mult))
                    link(dve.tensor_copy(hi_t[:, c0:c1], s))
                    dve.tensor_tensor(lo_t[:, c0:c1], s, hi_t[:, c0:c1], ALU.subtract)
            link(dve.tensor_scalar(stage_2[:, :], stage_2[:, :], W_SCALE, None, ALU.mult))
            link(dve.tensor_copy(w2_hi[:, :], stage_2[:, :]))
            link(dve.tensor_tensor(w2_lo[:, :], stage_2[:, :], w2_hi[:, :], ALU.subtract))
            for half, part in enumerate((w2_hi, w2_lo)):
                last = dve.tensor_copy(w2_both[:, :, CB * half:CB * half + CB],
                                       part[:, :].rearrange("p (j c) -> p j c", j=HT)[:, :, CA:C])
            last.then_inc(weights_ready, 1)

            def to_windows(t, slot, count):
                dve.wait_ge(x_loaded[slot], count)
                wait(dve, xt_full, 2 * t)
                for src, dst in ((xa[slot], xw_a), (xb[slot], xw_b)):
                    rows = src[:, :].rearrange("p (r c) -> p r c", r=WS)
                    wins = dst[:, :, 0:N].rearrange("p w (r c) -> p w r c", r=WS)
                    dve.tensor_copy(wins[:, 0:NW - 1], rows[:, :, SHIFT:SHIFT + T // WS - WS]
                                    .rearrange("p r (w c) -> p w r c", c=WS))
                    dve.tensor_copy(wins[:, NW - 1, :, 0:WS - SHIFT], rows[:, :, W - WS + SHIFT:W])
                    last = dve.tensor_copy(wins[:, NW - 1, :, WS - SHIFT:WS], rows[:, :, 0:SHIFT])
                last.then_inc(xw_ready, 1)

            def statistics(rows, full, t, banks, stats, half, chain):
                dve.wait_ge(full, 2 * t + half + 1)
                for g in (2 * half, 2 * half + 1):
                    last = dve.bn_stats(stats[0:rows, g, :],
                                        banks[0:rows, g // 2, (g % 2) * C:(g % 2 + 1) * C])
                if half:
                    last.then_inc(chain, 1)

            def mean_variance(rows, t, stats, mv, chain, done):
                dve.wait_ge(chain, t + 1)
                alone(dve, passed_dve)
                for g in range(4):
                    last = dve.bn_aggr(mv[0:rows, g, :], stats[0:rows, g, :])
                last.then_inc(done, 1)

            def probs_lo(u, pairs):
                for g in pairs:
                    dve.wait_ge(pt_hi, 4 * u + g + 1)
                    dve.tensor_tensor(pt_lo_sb[:, g, :, :], queries(bank("pt", g)),
                                      pt_hi_sb[:, g, :, :], ALU.subtract).then_inc(pt_lo, 1)

            def attended_lo(u):
                dve.wait_ge(o_hi, 2 * u + 2)
                dve.scalar_tensor_tensor(oa_lo[:, :].rearrange("p (b n) -> p b n", b=2),
                                         ps_o[:, :, 0:T // 2], bias[:, 3:4],
                                         oa_hi[:, :].rearrange("p (b n) -> p b n", b=2),
                                         ALU.add, ALU.subtract).then_inc(o_lo, 1)
                dve.scalar_tensor_tensor(o3[CB:128, :].rearrange("p (b n) -> p b n", b=2),
                                         ps_o[0:CB, :, T // 2:T], bias[0:CB, 4:5],
                                         o3[0:CB, :].rearrange("p (b n) -> p b n", b=2),
                                         ALU.add, ALU.subtract).then_inc(o_lo, 1)

            def normed_lo_1(t, halves):
                for i in halves:
                    dve.wait_ge(xn_hi, 2 * t + i + 1)
                    if i == 0:
                        dve.tensor_tensor(xna_lo[:, :, 0:N], tokens(bank("nt", 0)),
                                          xna_hi[:, :, 0:N], ALU.subtract).then_inc(xn_lo, 1)
                    else:
                        dve.tensor_tensor(xn3[CB:128, :, 0:N], tokens(bank("nt", 1)[0:CB, :]),
                                          xn3[0:CB, :, 0:N], ALU.subtract).then_inc(xn_lo, 1)

            def queries_keys_lo(t, tiles):
                for i in tiles:
                    dve.wait_ge(qk_hi, 3 * t + i + 1)
                    if i < 2:
                        hi, lo = ((q_hi, q_lo), (k_hi, k_lo))[i]
                        dve.scalar_tensor_tensor(lo[:, :], bank("qk", i)[:, 0:T], bias[:, i:i + 1],
                                                 hi[:, :], ALU.add, ALU.subtract
                                                 ).then_inc(qk_lo, 1)
                    else:
                        dve.scalar_tensor_tensor(q45_lo[:, :], bank("qk", 2)[0:64, 0:T],
                                                 bias[0:64, 2:3], q45_hi[:, :], ALU.add,
                                                 ALU.subtract)
                        dve.scalar_tensor_tensor(k45_lo[:, :], bank("qk", 2)[64:128, 0:T],
                                                 bias[64:128, 2:3], k45_hi[:, :], ALU.add,
                                                 ALU.subtract).then_inc(qk_lo, 1)

            def values_lo(t, i):
                dve.wait_ge(v_hi_done, 2 * t + i + 1)
                dve.tensor_tensor(v_lo[:, 2 * i:2 * i + 2, :], bank("v", i)[:, 0:2 * C]
                                  .rearrange("p (g c) -> p g c", g=2),
                                  v_hi[:, 2 * i:2 * i + 2, :], ALU.subtract
                                  ).then_inc(v_lo_done, 1)

            def normed_lo_2(u, halves):
                for i in halves:
                    dve.wait_ge(x2_hi, 2 * u + i + 1)
                    if i == 0:
                        dve.tensor_tensor(x2a_lo[:, :], bank("n2", 0)[:, 0:T], x2a_hi[:, :],
                                          ALU.subtract).then_inc(x2_lo, 1)
                    else:
                        dve.tensor_tensor(x23[CB:128, :], bank("n2", 1)[0:CB, 0:T], x23[0:CB, :],
                                          ALU.subtract).then_inc(x2_lo, 1)

            def windows(a):
                return a.rearrange("p (w n) -> p w n", n=N)

            def biased(t, p, kind):
                dve.wait_ge(s_full, PH * t + p + 1)
                wait(dve, p_exp, PH * (t - 1) + p + 1)
                dve.scalar_tensor_tensor(logits[:, p, :], ps_s[:, p, 0:T],
                                         HD ** -0.5 / (QKV_SCALE * QKV_SCALE),
                                         score_bias[:, kind, p, :], ALU.mult, ALU.add
                                         ).then_inc(s_biased, 1)

            def row_maxima(t, p):
                dve.wait_ge(s_biased, PH * t + p + 1)
                dve.tensor_reduce(row_max[:, p, :], windows(logits[:, p, :]), AX.X, ALU.max
                                  ).then_inc(s_max, 1)

            def row_sums(t, p):
                dve.wait_ge(p_exp, PH * t + p + 1)
                dve.tensor_reduce(row_sum[:, p, :], windows(expd[:, p, :]), AX.X, ALU.add
                                  ).then_inc(p_sum, 1)

            def inverse_sums(t, p):
                dve.wait_ge(p_sum, PH * t + p + 1)
                dve.reciprocal(row_inv[:, p, :], row_sum[:, p, :]).then_inc(p_inv, 1)

            def hidden_hi(m, j):
                dve.wait_ge(gelu_done, HT * m + j + 1)
                dve.tensor_copy(h_hi[:, j, :], gelu[:, j % 3, :]).then_inc(hh_done, 1)

            def hidden_lo(m, j):
                dve.wait_ge(hh_done, HT * m + j + 1)
                dve.tensor_tensor(h_lo[:, j, :], gelu[:, j % 3, :], h_hi[:, j, :],
                                  ALU.subtract).then_inc(h_ready, 1)

            def contracted_a(m, slot):
                dve.wait_ge(f2_full, 2 * m + 1)
                wait(dve, out_ready, m)
                dve.scalar_tensor_tensor(f2_a[:, :], bank("f2", 0)[:, 0:T], 1.0 / W_SCALE,
                                         x1_a[slot][:, :], ALU.mult, ALU.add).then_inc(f2_sum, 1)

            def contracted_b(m, slot):
                dve.wait_ge(f2_full, 2 * m + 2)
                dve.scalar_tensor_tensor(f2_b[:, :], bank("f2", 1)[0:CB, 0:T], 1.0 / W_SCALE,
                                         x1_b[slot][:, :], ALU.mult, ALU.add
                                         ).then_inc(f2_half, 1)
                dve.wait_ge(f2_half, m + 1)
                dve.scalar_tensor_tensor(f2_b[:, :], bank("f2", 1)[CB:128, 0:T], 1.0 / W_SCALE,
                                         f2_b[:, :], ALU.mult, ALU.add).then_inc(f2_sum, 1)

            def iteration(t, slot, kind, stages=(0, 1, 2), count=None):
                front, back, mlp = (n in stages for n in range(3))
                u, m = t - 1, t - 2
                if mlp:
                    hidden_hi(m, 0)
                if front:
                    statistics(128, xt_full, t, ps_s, stats1, 0, stat1_chain)
                if mlp:
                    hidden_lo(m, 0)
                if back:
                    probs_lo(u, (0,))
                if front:
                    statistics(128, xt_full, t, ps_s, stats1, 1, stat1_chain)
                if back:
                    probs_lo(u, (1,))
                if front:
                    mean_variance(128, t, stats1, mv1, stat1_chain, aggr1)
                if mlp:
                    for i in (1, 2):
                        hidden_hi(m, i)
                    hidden_lo(m, 1)
                if back:
                    probs_lo(u, (2, 3))
                if mlp:
                    hidden_lo(m, 2)
                    hidden_hi(m, 3)
                    hidden_lo(m, 3)
                if back:
                    attended_lo(u)
                if front:
                    normed_lo_1(t, (0,))
                if mlp:
                    hidden_hi(m, 4)
                if front:
                    normed_lo_1(t, (1,))
                if mlp:
                    hidden_hi(m, 5)
                if front:
                    queries_keys_lo(t, (0, 1))
                if mlp:
                    hidden_lo(m, 4)
                if front:
                    queries_keys_lo(t, (2,))
                if back:
                    statistics(XG, x1t_full, u, ps_o, stats2, 0, stat2_chain)
                    statistics(XG, x1t_full, u, ps_o, stats2, 1, stat2_chain)
                if front:
                    biased(t, 0, kind)
                if back:
                    mean_variance(XG, u, stats2, mv2, stat2_chain, aggr2)
                if mlp:
                    hidden_lo(m, 5)
                if front:
                    values_lo(t, 0)
                    biased(t, 1, kind)
                    row_maxima(t, 0)
                    biased(t, 2, kind)
                    for i in (1, 2):
                        row_maxima(t, i)
                if count is not None:
                    to_windows(t + 1, 1 - slot, count)
                if front:
                    for i in (0, 1):
                        row_sums(t, i)
                if back:
                    normed_lo_2(u, (0, 1))
                if front:
                    inverse_sums(t, 0)
                    row_sums(t, 2)
                    for i in (1, 2):
                        inverse_sums(t, i)
                if mlp:
                    contracted_a(m, slot)
                if front:
                    values_lo(t, 1)
                if mlp:
                    contracted_b(m, slot)

            to_windows(0, 0, 64)

            def pairs(t, kind):
                iteration(t, 0, kind, count=32 * t + 64)
                iteration(t + 1, 1, kind, count=32 * t + 128)

            iteration(0, 0, 0, (0,), count=64)
            iteration(1, 1, 0, (0, 1), count=128)
            pairs(2, 0)
            with dve.Fori(4, PLAIN, 2) as t:
                pairs(t, 0)
            with dve.Fori(PLAIN, STRIPS - 2, 2) as t:
                pairs(t, 1)
            iteration(STRIPS - 2, 0, 1, count=32 * STRIPS)
            iteration(STRIPS - 1, 1, 1)
            iteration(STRIPS, 0, 1, (1, 2))
            iteration(STRIPS + 1, 1, 1, (2,))

        @block.gpsimd
        def _(pool):
            pool.memset(eps_sb[:, :], EPS)
            pool.memset(power_sb[:, :], -0.5)
            pool.memset(minus_sb[:, :], -1.0)
            pool.memset(warm[:, :], 0.0)
            pool.memset(probs[:, :, :, :], 0.0).then_inc(consts_ready, 1)
            pool.wait_ge(consts_ready, 1)

            def inverse_deviation(rows, t, aggr, mv, var, rstd, shift, chain, ready):
                pool.wait_ge(aggr, t + 1)
                pool.tensor_tensor(var[0:rows, :], mv[0:rows, :, 1], eps_sb[0:rows, :], ALU.add)
                pool.tensor_tensor(shift[0:rows, :], mv[0:rows, :, 0], minus_sb[0:rows, :],
                                   ALU.mult).then_inc(pool_chain, 1)
                pool.wait_ge(pool_chain, chain + 1)
                pool.tensor_tensor(rstd[0:rows, :], var[0:rows, :], power_sb[0:rows, :],
                                   ALU.pow).then_inc(pool_chain, 1)
                pool.wait_ge(pool_chain, chain + 2)
                pool.tensor_tensor(shift[0:rows, :], shift[0:rows, :], rstd[0:rows, :],
                                   ALU.mult).then_inc(ready, 1)

            def residual(u, slot):
                wait(pool, f2_sum, 2 * (u - 1))
                pool.wait_ge(pj_out, 2 * u + 2)
                for pj, xs, x1 in ((pj_a, xa[slot], x1_a[slot]), (pj_b, xb[slot], x1_b[slot])):
                    pj_r, x_r, x1_r = (a[:, :].rearrange("p (r c) -> p r c", r=WS)
                                       for a in (pj, xs, x1))
                    pool.tensor_tensor(x1_r[:, :, SHIFT:W], pj_r[:, :, 0:CUT], x_r[:, :, SHIFT:W],
                                       ALU.add)
                    last = pool.tensor_tensor(x1_r[:, :, 0:SHIFT], pj_r[:, :, CUT:W],
                                              x_r[:, :, 0:SHIFT], ALU.add)
                last.then_inc(x1_ready, 1)

            def subtract_max(t, p):
                pool.wait_ge(s_max, PH * t + p + 1)
                rows = logits[:, p, :].rearrange("p (w n) -> p w n", n=N)
                pool.tensor_tensor(rows, rows, row_max[:, p, :].unsqueeze(2)
                                   .to_broadcast([128, NW, N]), ALU.subtract
                                   ).then_inc(s_shifted, 1)

            def normalise(t, p):
                pool.wait_ge(p_inv, PH * t + p + 1)
                wait(pool, pt_full, 4 * t)
                pool.tensor_tensor(probs[:, p, :, 0:N],
                                   expd[:, p, :].rearrange("p (w n) -> p w n", n=N),
                                   row_inv[:, p, :].unsqueeze(2).to_broadcast([128, NW, N]),
                                   ALU.mult).then_inc(p_ready, 1)

            def finish(m, halves):
                for i in halves:
                    rows, f2, dst = ((CA, f2_a, out_a), (CB, f2_b, out_b))[i]
                    pool.wait_ge(f2_sum, 2 * m + i + 1)
                    if i == 0:
                        wait(pool, out_stored, 64 * m)
                    last = pool.tensor_tensor(dst[:, :], f2[:, :], b_fc2_sb[0:rows, i:i + 1]
                                              .to_broadcast([rows, T]), ALU.add)
                if i == 1:
                    last.then_inc(out_ready, 1)

            def iteration(t, slot, stages=(0, 1, 2), chain=0):
                front, back, mlp = (n in stages for n in range(3))
                u, m = t - 1, t - 2
                if front:
                    inverse_deviation(128, t, aggr1, mv1, var1, rstd1, shift1, chain, rstd1_ready)
                    chain = chain + 2
                if back:
                    residual(u, 1 - slot)
                    inverse_deviation(XG, u, aggr2, mv2, var2, rstd2, shift2, chain, rstd2_ready)
                if front:
                    for i in (0, 1, 2):
                        subtract_max(t, i)
                    for i in (0, 1, 2):
                        normalise(t, i)
                if mlp:
                    finish(m, (0, 1))

            iteration(0, 0, (0,))
            iteration(1, 1, (0, 1), chain=2)
            iteration(2, 0, chain=6)
            iteration(3, 1, chain=10)
            with pool.Fori(4, STRIPS, 2) as t:
                iteration(t, 0, chain=4 * t - 2)
                iteration(t + 1, 1, chain=4 * t + 2)
            iteration(STRIPS, 0, (1, 2), chain=4 * STRIPS - 2)
            iteration(STRIPS + 1, 1, (2,))


def kernel(x, L0_conv_qkv_w, L0_conv_qkv_b, L0_conv_proj_w, L0_conv_proj_b, L0_conv_rpb_table,
           L0_conv_norm1_g, L0_conv_norm1_b, L0_conv_norm2_g, L0_conv_norm2_b,
           L0_conv_fc1_w, L0_conv_fc1_b, L0_conv_fc2_w, L0_conv_fc2_b):
    import numpy as np
    import concourse.bacc as bacc
    from concourse.bass_utils import run_bass_kernel_spmd as run

    def lay(a):
        return np.ascontiguousarray(a)

    x = np.asarray(x)
    qkv_w, qkv_b = np.asarray(L0_conv_qkv_w), np.asarray(L0_conv_qkv_b)

    def two_columns(v):
        v = np.asarray(v)
        return lay(np.stack([v[:CA], np.concatenate([v[CA:], v[CA:]])], axis=1))

    order = np.concatenate([np.arange(0, CA), np.arange(C, C + CA),
                            np.arange(CA, C), np.arange(C + CA, 2 * C)])
    r, c = np.divmod(np.arange(N), WS)
    index = (r[:, None] - r[None, :] + WS - 1) * (2 * WS - 1) + (c[:, None] - c[None, :] + WS - 1)
    gathered = np.asarray(L0_conv_rpb_table)[index]
    rpb = np.zeros((128, PH, N), np.float32)
    for h in range(HEADS):
        rpb[NP * (h % 2):NP * (h % 2) + N, h // 2] = gathered[:, :, h]
    late_r, late_c = r >= WS - SHIFT, c >= WS - SHIFT
    mask = np.zeros((128, 2, NW, N), np.float32)
    for kind in range(2):
        for w in range(NW):
            apart = np.zeros((N, N), bool)
            if kind == 1:
                apart |= late_r[:, None] != late_r[None, :]
            if w == NW - 1:
                apart |= late_c[:, None] != late_c[None, :]
            for half in (0, NP):
                mask[half:half + N, kind, w] = np.where(apart, np.float32(-100), np.float32(0))

    fc2_t = np.asarray(L0_conv_fc2_w).T
    arrays = {
        "x": lay(x.reshape(B, C, H * W)),
        "w_qk": lay(qkv_w[order].T),
        "w_v": lay(qkv_w[2 * C:].T),
        "w_proj": lay(np.asarray(L0_conv_proj_w).T),
        "w_fc1": lay(np.asarray(L0_conv_fc1_w).T),
        "w_fc2": lay(fc2_t.reshape(HT, 128, C).transpose(1, 0, 2).reshape(128, HT * C)),
        "b_qk": lay(qkv_b[order].reshape(3, 128).T),
        "b_v": two_columns(qkv_b[2 * C:]),
        "b_proj": two_columns(L0_conv_proj_b),
        "b_fc1": lay(np.asarray(L0_conv_fc1_b).reshape(HT, 128).T),
        "b_fc2": two_columns(L0_conv_fc2_b),
        "g1": two_columns(L0_conv_norm1_g),
        "beta1": two_columns(L0_conv_norm1_b),
        "g2": two_columns(L0_conv_norm2_g),
        "beta2": two_columns(L0_conv_norm2_b),
        "rpb": lay(rpb.reshape(128, PH * N)),
        "mask": lay(mask.reshape(128, 2, T)),
        "ident": np.eye(128, dtype=np.float32),
    }
    nc = bacc.Bacc("TRN2", target_bir_lowering=False, num_devices=1)
    args = [nc.dram_tensor(f"in_{k}", a.shape, mybir.dt.from_np(a.dtype), kind="ExternalInput").ap()
            for k, a in arrays.items()]
    result = nc.dram_tensor("out_dram", (B, C, H * W), mybir.dt.float32, kind="ExternalOutput").ap()
    swin_block(nc, *args, result)
    r = run(nc, [{f"in_{k}": a for k, a in arrays.items()}], core_ids=[0])
    return r.results[0]["out_dram"].reshape(B, C, H, W)
```
